# Optimizing a Trainium2 kernel written in Bass

```python
import numpy as np
import jax
import jax.numpy as jnp

def _softmax(x, axis=-1):
    return jax.nn.softmax(x, axis=axis)

def _gelu(x):
    return jax.nn.gelu(x, approximate=True)

def _silu(x):
    return jax.nn.silu(x)

def _sigmoid(x):
    return jax.nn.sigmoid(x)

def _layernorm(x, axis=-1, eps=1e-05):
    m = jnp.mean(x, axis=axis, keepdims=True)
    v = jnp.var(x, axis=axis, keepdims=True)
    return (x - m) / jnp.sqrt(v + eps)

def _scatter_add(tgt, idx, src, axis=0):
    return tgt.at[idx].add(src)

def _segment_sum(src, seg, n):
    return jax.ops.segment_sum(src, seg, n)
kernel_name = 'mk_xattn_seq_d1_seqx_r4_9a088f'

def setup_inputs(seed: int=0):
    np.random.seed(seed)
    _w = jnp.asarray

    def _rec_inputs():
        import jax
        import jax.numpy as jnp
        _rk = jax.random.key(seed)
        x = 7.22e-05 + 1 * jax.random.normal(jax.random.fold_in(_rk, 1), (2, 1024, 256), jnp.float32)
        _lenS = 1024 - jax.random.randint(jax.random.fold_in(_rk, 7), (2,), 0, max(1, 1024 // 4) + 1, jnp.int32)
        _lenS2 = 64 - jax.random.randint(jax.random.fold_in(_rk, 8), (2,), 0, max(1, 64 // 4) + 1, jnp.int32)
        _ctx_768P = jax.random.normal(jax.random.fold_in(_rk, 11), (2, 16, 192), jnp.float32)
        _ctx_768c = jax.random.dirichlet(jax.random.fold_in(_rk, 511), 0.3 * jnp.ones((16,), jnp.float32), (2, 64))
        _ctx_768t = jnp.einsum('bsk,bkd->bsd', _ctx_768c, _ctx_768P)
        _ctx_768t = _ctx_768t * jax.lax.rsqrt(jnp.mean(jnp.square(_ctx_768t)) + 1e-12) * 0.953939
        ctx_768 = -0.00055796 + 0.999787 * (_ctx_768t + 0.3 * jax.random.normal(jax.random.fold_in(_rk, 611), (2, 64, 192), jnp.float32))
        return (x, ctx_768)
    x, ctx_768 = _rec_inputs()

    def _L0_xattn_setup():
        import jax, jax.numpy as jnp
        import numpy as np
        D_MODEL = 256
        D_COND = 192
        N_HEADS = 16
        D_HEAD = 64
        D_ATTN = N_HEADS * D_HEAD
        D_FF = 4 * D_MODEL

        def _layernorm(x, g, b, eps=1e-05):
            mu = jnp.mean(x, axis=-1, keepdims=True)
            var = jnp.var(x, axis=-1, keepdims=True)
            return (x - mu) * jax.lax.rsqrt(var + eps) * g + b

        def _attention(xq, xkv, wq, wk, wv, wo, bo):
            B, S, _ = xq.shape
            T = xkv.shape[1]
            q = (xq @ wq).reshape(B, S, N_HEADS, D_HEAD)
            k = (xkv @ wk).reshape(B, T, N_HEADS, D_HEAD)
            v = (xkv @ wv).reshape(B, T, N_HEADS, D_HEAD)
            scale = D_HEAD ** (-0.5)
            attn = jnp.einsum('bihd,bjhd->bhij', q, k) * scale
            attn = jax.nn.softmax(attn, axis=-1)
            out = jnp.einsum('bhij,bjhd->bihd', attn, v).reshape(B, S, D_ATTN)
            return out @ wo + bo
        key = jax.random.key(seed)
        ks = jax.random.split(key, 16)
        B, S, T = (8, 256, 64)
        n = jax.random.normal
        inp = {'x': n(ks[0], (B, S, D_MODEL), jnp.float32), 'cond_emb': n(ks[1], (B, T, D_COND), jnp.float32), 'ln1_g': jnp.ones((D_MODEL,), jnp.float32), 'ln1_b': jnp.zeros((D_MODEL,), jnp.float32), 'ln2_g': jnp.ones((D_MODEL,), jnp.float32), 'ln2_b': jnp.zeros((D_MODEL,), jnp.float32), 'ln3_g': jnp.ones((D_MODEL,), jnp.float32), 'ln3_b': jnp.zeros((D_MODEL,), jnp.float32), 'sa_wq': n(ks[2], (D_MODEL, D_ATTN), jnp.float32) * D_MODEL ** (-0.5), 'sa_wk': n(ks[3], (D_MODEL, D_ATTN), jnp.float32) * D_MODEL ** (-0.5), 'sa_wv': n(ks[4], (D_MODEL, D_ATTN), jnp.float32) * D_MODEL ** (-0.5), 'sa_wo': n(ks[5], (D_ATTN, D_MODEL), jnp.float32) * D_ATTN ** (-0.5), 'sa_bo': jnp.zeros((D_MODEL,), jnp.float32), 'ca_wq': n(ks[6], (D_MODEL, D_ATTN), jnp.float32) * D_MODEL ** (-0.5), 'ca_wk': n(ks[7], (D_COND, D_ATTN), jnp.float32) * D_COND ** (-0.5), 'ca_wv': n(ks[8], (D_COND, D_ATTN), jnp.float32) * D_COND ** (-0.5), 'ca_wo': n(ks[9], (D_ATTN, D_MODEL), jnp.float32) * D_ATTN ** (-0.5), 'ca_bo': jnp.zeros((D_MODEL,), jnp.float32), 'ff_w1': n(ks[10], (D_MODEL, 2 * D_FF), jnp.float32) * D_MODEL ** (-0.5), 'ff_b1': jnp.zeros((2 * D_FF,), jnp.float32), 'ff_w2': n(ks[11], (D_FF, D_MODEL), jnp.float32) * D_FF ** (-0.5), 'ff_b2': jnp.zeros((D_MODEL,), jnp.float32)}
        return inp
    _L0_xattn_all = _L0_xattn_setup()
    _L0_xattn_in = {k: v for k, v in _L0_xattn_all.items() if k in ('ln1_g', 'ln1_b', 'ln2_g', 'ln2_b', 'ln3_g', 'ln3_b', 'sa_wq', 'sa_wk', 'sa_wv', 'sa_wo', 'sa_bo', 'ca_wq', 'ca_wk', 'ca_wv', 'ca_wo', 'ca_bo', 'ff_w1', 'ff_b1', 'ff_w2', 'ff_b2')}
    del _L0_xattn_all
    return {'x': x, 'ctx_768': ctx_768, 'L0_xattn_ln1_g': _L0_xattn_in['ln1_g'], 'L0_xattn_ln1_b': _L0_xattn_in['ln1_b'], 'L0_xattn_ln2_g': _L0_xattn_in['ln2_g'], 'L0_xattn_ln2_b': _L0_xattn_in['ln2_b'], 'L0_xattn_ln3_g': _L0_xattn_in['ln3_g'], 'L0_xattn_ln3_b': _L0_xattn_in['ln3_b'], 'L0_xattn_sa_wq': _L0_xattn_in['sa_wq'], 'L0_xattn_sa_wk': _L0_xattn_in['sa_wk'], 'L0_xattn_sa_wv': _L0_xattn_in['sa_wv'], 'L0_xattn_sa_wo': _L0_xattn_in['sa_wo'], 'L0_xattn_sa_bo': _L0_xattn_in['sa_bo'], 'L0_xattn_ca_wq': _L0_xattn_in['ca_wq'], 'L0_xattn_ca_wk': _L0_xattn_in['ca_wk'], 'L0_xattn_ca_wv': _L0_xattn_in['ca_wv'], 'L0_xattn_ca_wo': _L0_xattn_in['ca_wo'], 'L0_xattn_ca_bo': _L0_xattn_in['ca_bo'], 'L0_xattn_ff_w1': _L0_xattn_in['ff_w1'], 'L0_xattn_ff_b1': _L0_xattn_in['ff_b1'], 'L0_xattn_ff_w2': _L0_xattn_in['ff_w2'], 'L0_xattn_ff_b2': _L0_xattn_in['ff_b2']}

def reference(x, ctx_768, L0_xattn_ln1_g, L0_xattn_ln1_b, L0_xattn_ln2_g, L0_xattn_ln2_b, L0_xattn_ln3_g, L0_xattn_ln3_b, L0_xattn_sa_wq, L0_xattn_sa_wk, L0_xattn_sa_wv, L0_xattn_sa_wo, L0_xattn_sa_bo, L0_xattn_ca_wq, L0_xattn_ca_wk, L0_xattn_ca_wv, L0_xattn_ca_wo, L0_xattn_ca_bo, L0_xattn_ff_w1, L0_xattn_ff_b1, L0_xattn_ff_w2, L0_xattn_ff_b2):
    import jax
    import jax.numpy as jnp

    def _L0_xattn_ref(x, cond_emb, ln1_g, ln1_b, ln2_g, ln2_b, ln3_g, ln3_b, sa_wq, sa_wk, sa_wv, sa_wo, sa_bo, ca_wq, ca_wk, ca_wv, ca_wo, ca_bo, ff_w1, ff_b1, ff_w2, ff_b2):
        import jax, jax.numpy as jnp
        import numpy as np
        D_MODEL = 256
        D_COND = 192
        N_HEADS = 16
        D_HEAD = 64
        D_ATTN = N_HEADS * D_HEAD
        D_FF = 4 * D_MODEL

        def _layernorm(x, g, b, eps=1e-05):
            mu = jnp.mean(x, axis=-1, keepdims=True)
            var = jnp.var(x, axis=-1, keepdims=True)
            return (x - mu) * jax.lax.rsqrt(var + eps) * g + b

        def _attention(xq, xkv, wq, wk, wv, wo, bo):
            B, S, _ = xq.shape
            T = xkv.shape[1]
            q = (xq @ wq).reshape(B, S, N_HEADS, D_HEAD)
            k = (xkv @ wk).reshape(B, T, N_HEADS, D_HEAD)
            v = (xkv @ wv).reshape(B, T, N_HEADS, D_HEAD)
            scale = D_HEAD ** (-0.5)
            attn = jnp.einsum('bihd,bjhd->bhij', q, k) * scale
            attn = jax.nn.softmax(attn, axis=-1)
            out = jnp.einsum('bhij,bjhd->bihd', attn, v).reshape(B, S, D_ATTN)
            return out @ wo + bo
        h = _layernorm(x, ln1_g, ln1_b)
        x = _attention(h, h, sa_wq, sa_wk, sa_wv, sa_wo, sa_bo) + x
        h = _layernorm(x, ln2_g, ln2_b)
        x = _attention(h, cond_emb, ca_wq, ca_wk, ca_wv, ca_wo, ca_bo) + x
        h = _layernorm(x, ln3_g, ln3_b)
        p = h @ ff_w1 + ff_b1
        a, gate = (p[..., :D_FF], p[..., D_FF:])
        h = a * jax.nn.gelu(gate, approximate=False) @ ff_w2 + ff_b2
        return h + x
    x = _L0_xattn_ref(x, ctx_768, L0_xattn_ln1_g, L0_xattn_ln1_b, L0_xattn_ln2_g, L0_xattn_ln2_b, L0_xattn_ln3_g, L0_xattn_ln3_b, L0_xattn_sa_wq, L0_xattn_sa_wk, L0_xattn_sa_wv, L0_xattn_sa_wo, L0_xattn_sa_bo, L0_xattn_ca_wq, L0_xattn_ca_wk, L0_xattn_ca_wv, L0_xattn_ca_wo, L0_xattn_ca_bo, L0_xattn_ff_w1, L0_xattn_ff_b1, L0_xattn_ff_w2, L0_xattn_ff_b2)
    return x

_drawn_inputs = setup_inputs


def setup_inputs(seed=0):
    import zlib

    import numpy as np

    out = dict(_drawn_inputs(seed))
    spreads = {'L0_xattn_ln1_g': (1.0, 0.2),
     'L0_xattn_ln1_b': (0.0, 0.1),
     'L0_xattn_ln2_g': (1.0, 0.2),
     'L0_xattn_ln2_b': (0.0, 0.338),
     'L0_xattn_ln3_g': (1.0, 0.2),
     'L0_xattn_ln3_b': (0.0, 0.1),
     'L0_xattn_sa_bo': (0.0, 0.1),
     'L0_xattn_ca_bo': (0.0, 0.1),
     'L0_xattn_ff_b1': (0.0, 0.1),
     'L0_xattn_ff_b2': (0.0, 0.1)}
    factors = {}
    for name, (base, spread) in spreads.items():
        noise = np.random.default_rng([zlib.crc32(name.encode()), seed]).standard_normal(out[name].shape)
        drawn = base * np.exp(spread * noise) if base else spread * noise
        out[name] = jnp.asarray(drawn.astype(out[name].dtype))
    for name, factor in factors.items():
        out[name] = (out[name] * factor).astype(out[name].dtype)
    return out
```

```python
from contextlib import ExitStack

import concourse.bass as bass
from concourse import mybir

F32 = mybir.dt.float32
F32R = mybir.dt.float32r
ALU = mybir.AluOpType
ACT = mybir.ActivationFunctionType
AX = mybir.AxisListType.X
ds = bass.ds

P = 128
BANK = 512
EPS = 1e-5


def build_block(nc, x, cond, ln1_g, ln1_b, ln2_g, ln2_b, ln3_g, ln3_b, sa_wq, sa_wk, sa_wv, sa_wo, sa_bo,
                ca_wq, ca_wk, ca_wv, ca_wo, ca_bo, ff_w1, ff_b1, ff_w2, ff_b2, out):
    B, S, D = x.shape
    T, DC = cond.shape[1:]
    DA = sa_wq.shape[1]
    FF = ff_w2.shape[0]
    DH = 64
    NH = DA // DH
    NP = NH // 2
    NT = S // P
    KD = D // P
    NF = FF // P
    UP = 4
    NU = NP * UP
    UT = 4
    NPT = 4
    SCALE = float(DH) ** -0.5
    assert (B, S, D, T, DC, DA, FF) == (2, 1024, 256, 64, 192, 1024, 1024)

    with ExitStack() as ctx:
        def sb(name, shape, dt=F32):
            return ctx.enter_context(nc.sbuf_tensor(name, shape, dt))

        def sem(name):
            return ctx.enter_context(nc.semaphore(name))

        X = sb("X", [P, NT, D])
        hT = [sb("hT_hi", [P, KD, S], F32R), sb("hT_lo", [P, KD, S], F32R)]
        PR = sb("PR", [P, 2, UT, S])
        PT = [sb("PT_hi", [P, NPT, BANK], F32R), sb("PT_lo", [P, NPT, BANK], F32R)]
        QKT = sb("QKT", [P, 4, S], F32R)
        QKS = sb("QKS", [P, 6, S], F32R)
        VT = sb("VT", [P, 2, NT, P], F32R)
        VS = [sb(f"VS{h}", [P, NT, P], F32R) for h in range(2)]
        OT = [sb("OT_hi", [P, BANK], F32R), sb("OT_lo", [P, BANK], F32R)]
        w_raw = sb("w_raw", [P, 3, KD, P])
        w_s = [sb("w_hi", [P, 3, KD, P], F32R), sb("w_lo", [P, 3, KD, P], F32R)]
        wo_raw = [sb(f"wo_raw{h}", [P, D]) for h in range(2)]
        wo_s = [[sb(f"wo_hi{h}", [P, D], F32R), sb(f"wo_lo{h}", [P, D], F32R)] for h in range(2)]
        W1 = [sb("W1_hi", [P, KD, 2 * FF], F32R), sb("W1_lo", [P, KD, 2 * FF], F32R)]
        W2 = [sb("W2_hi", [P, NF, D], F32R), sb("W2_lo", [P, NF, D], F32R)]
        ident = sb("ident", [P, P])
        bias_row = sb("bias_row", [P, 3, D])
        gb = sb("gb", [P, 3, 2, KD])
        b1 = sb("b1", [P, 2 * NF])
        f_raw = sb("f_raw", [P, 2, BANK])
        cnd = sb("cnd", [P, DC])
        cndT = sb("cndT", [P, 2, P])
        st = sb("st", [P, NT, 6])
        mv = sb("mv", [P, NT, 2])
        sd = sb("sd", [P, NT])
        rs = sb("rs", [P, NT])
        nmax = sb("nmax", [P, 4])
        den = sb("den", [P, 2, UT])
        rden = sb("rden", [P, 2, UT])
        cmax = sb("cmax", [P, 2, NH])
        csum = sb("csum", [P, 2, NH])
        crec = sb("crec", [P, 2, NH])

        M_d = nc.dram_tensor("scratch_m", [2, B, P, KD, DA], F32, kind="Internal").ap()
        VW_d = nc.dram_tensor("scratch_vw", [2, B, P, NP, D], F32, kind="Internal").ap()

        SC = [ctx.enter_context(nc.psum_tensor(f"SC{i}", [P, 2 * BANK], F32)) for i in range(2)]
        TP = [ctx.enter_context(nc.psum_tensor(f"TP{i}", [P, BANK], F32)) for i in range(2)]
        PV = ctx.enter_context(nc.psum_tensor("PV", [P, BANK], F32))
        MISC = ctx.enter_context(nc.psum_tensor("MISC", [P, BANK], F32))

        prf = PR[:, :, :, :].rearrange("p a b n -> p (a b) n")
        z = PR[:, 0, 0:2, :].rearrange("p a n -> p (a n)").rearrange("p (t d) -> p t d", d=D)
        h32 = PR[:, 0, 2:4, :]
        wk_a, wk_b, wv_a, wv_b = prf[:, 0, :], prf[0:DC - P, 1, :], prf[:, 2, :], prf[0:DC - P, 3, :]
        kblk = prf[:, 4:6, :].rearrange("p a n -> p (a n)").rearrange("p (n b c) -> p n b c", n=NP, b=B)
        vblk = prf[:, 6:8, :].rearrange("p a n -> p (a n)").rearrange("p (n b c) -> p n b c", n=NP, b=B)
        caq = prf[:, 0:2, :]
        wqT = prf[:, 2:4, :].rearrange("p a n -> p (a n)").rearrange("p (n c) -> p n c", c=D)
        E = [PR[:, 1, i, :] for i in range(4)]
        G = [PR[:, 0, i, 0:BANK] for i in range(2)]
        U32 = [PR[:, 0, 2 + i, 0:BANK] for i in range(2)]
        Mx = [QKT[:, 0:2, :], QKT[:, 2:4, :]]
        vwf = QKS[:, 0:4, :].rearrange("p a n -> p (a n)").rearrange("p (l n d) -> p l n d", l=2, d=D)
        VWx = [vwf[:, 0], vwf[:, 1]]

        m_x = sem("m_x"); m_out = sem("m_out"); m_cst = sem("m_cst"); m_cnd = sem("m_cnd")
        m_kv = sem("m_kv"); m_caq = sem("m_caq"); m_cao = sem("m_cao"); m_scr = [sem(f"m_scr{i}") for i in range(4)]
        m_w = sem("m_w"); m_wo = [sem("m_wo0"), sem("m_wo1")]; m_f = [sem("m_f0"), sem("m_f1")]
        m_qk = [sem("m_qk0"), sem("m_qk1")]; m_v = [sem("m_v0"), sem("m_v1")]
        m_m = sem("m_m"); m_vw = sem("m_vw")
        waited = sem("waited")
        p_id = sem("p_id"); p_blk = sem("p_blk")
        p_w = sem("p_w"); p_wo = [sem("p_wo0"), sem("p_wo1")]; p_f = sem("p_f"); p_wh = sem("p_wh")
        p_xb = sem("p_xb"); p_cn = sem("p_cn")
        s_pre = sem("s_pre"); d_pre = sem("d_pre"); a_pre = sem("a_pre")
        d_st = sem("d_st"); d_mv = sem("d_mv"); a_sd = sem("a_sd"); d_rs = sem("d_rs"); d_z = sem("d_z")
        s_tr = sem("s_tr"); d_h = sem("d_h"); a_hh = sem("a_hh"); d_hl = sem("d_hl")
        s_sc = sem("s_sc"); d_max = sem("d_max"); a_exp = sem("a_exp"); d_rd = sem("d_rd")
        s_pt = sem("s_pt"); a_ph = sem("a_ph"); d_pl = sem("d_pl"); s_pv = sem("s_pv")
        a_oh = sem("a_oh"); d_ol = sem("d_ol"); s_op = sem("s_op"); d_x = sem("d_x")
        s_qkv = sem("s_qkv"); a_qkv = sem("a_qkv"); d_qkv = sem("d_qkv")
        s_cs = sem("s_cs"); d_cm = sem("d_cm"); d_cs = sem("d_cs"); a_ce = sem("a_ce")
        d_csum = sem("d_csum"); d_cr = sem("d_cr"); s_ct = sem("s_ct"); a_ch = sem("a_ch"); d_cl = sem("d_cl")
        s_co = sem("s_co"); d_cx = sem("d_cx")
        s_ff = sem("s_ff"); a_g = sem("a_g"); d_u = sem("d_u"); a_uh = sem("a_uh"); d_ul = sem("d_ul")
        s_w2 = sem("s_w2"); d_fx = sem("d_fx")

        TERMS = [(0, 0), (0, 1), (1, 0)]

        PROJ = [("q", 0), ("k", 0), ("k", 1), ("q", 1), ("v", 0), ("v", 1)]
        NQ = len(PROJ)
        FW_CHUNKS = 12

        def wait_apart(eng, signal, value):
            eng.wait_ge(signal, value)
            eng.sem_inc(waited, 1)

        block = ctx.enter_context(nc.Block())

        @block.sync
        def _(sp):
            def move(to, of, signal):
                sp.dma_start(to.bitcast(F32), of.bitcast(F32)).then_inc(signal, 16)

            def load_w(p):
                for m, w in enumerate((sa_wq, sa_wk, sa_wv)):
                    sp.dma_start(w_raw[:, m, :, :], w.rearrange("(k p) n -> p k n", p=P)[:, :, ds(p * P, P)])\
                      .then_inc(m_w, 16)

            def load_wo(h, p):
                for half in range(2):
                    sp.dma_start(wo_raw[h][64 * half:64 * half + 64, :], sa_wo[ds(p * P + 64 * h, 64), :])\
                      .then_inc(m_wo[h], 16)

            def place_qk(h):
                r = slice(64 * h, 64 * h + 64)
                for slot, (top, bottom) in enumerate(((0, 1), (2, 2), (3, 3))):
                    move(QKS[0:64, 3 * h + slot, :], QKT[r, top, :], m_qk[h])
                    move(QKS[64:128, 3 * h + slot, :], QKT[r, bottom, :], m_qk[h])

            def place_v(h):
                move(VS[h][:, :, :], VT[:, h, :, :], m_v[h])

            cw = lambda w: (w[0:P, :], w[P:DC, :])
            sp.dma_start(cnd[:, :], cond.rearrange("b t c -> (b t) c")).then_inc(m_cnd, 16)
            for dst, src in ((wk_a, cw(ca_wk)[0]), (wk_b, cw(ca_wk)[1]), (wv_a, cw(ca_wv)[0]), (wv_b, cw(ca_wv)[1])):
                sp.dma_start(dst, src).then_inc(m_kv, 16)
            sp.dma_start(X[:, :, :], ca_wo.rearrange("(n p) d -> p n d", p=P)).then_inc(m_cao, 16)
            for i, v in enumerate((sa_bo, ca_bo, ff_b2)):
                sp.dma_start(bias_row[:, i, :], v.rearrange("(a n) -> a n", a=1).broadcast_to([P, D])).then_inc(m_cst, 16)
            with nc.allow_non_contiguous_dma(reason="small vectors by feature"):
                for i, (g_, b_) in enumerate(((ln1_g, ln1_b), (ln2_g, ln2_b), (ln3_g, ln3_b))):
                    sp.dma_start(gb[:, i, 0, :], g_.rearrange("(k p) -> p k", p=P)).then_inc(m_cst, 16)
                    sp.dma_start(gb[:, i, 1, :], b_.rearrange("(k p) -> p k", p=P)).then_inc(m_cst, 16)
                sp.dma_start(b1[:, :], ff_b1.rearrange("(k p) -> p k", p=P)).then_inc(m_cst, 16)
            sp.wait_ge(s_pre, 3)
            sp.dma_start(caq, ca_wq.rearrange("(k p) n -> p k n", p=P)).then_inc(m_caq, 16)
            load_w(0)
            load_wo(0, 0)
            load_wo(1, 0)
            for i in range(16):
                sp.wait_ge(d_pre, 10 + i)
                for l in range(2):
                    if i < 8:
                        src = PT[l][:, i % NPT, :].rearrange("p (n b c) -> p b n c", n=2, b=B)
                        for bb in range(B):
                            move(M_d[l, bb, :, i // 4, 256 * (i % 4):256 * (i % 4) + 256]
                                 .rearrange("p (n c) -> p n c", n=2), src[:, bb], m_scr[i % NPT])
                    else:
                        for bb in range(B):
                            move(VW_d[l, bb, :, i - 8, :], PT[l][:, i % NPT, 256 * bb:256 * bb + 256], m_scr[i % NPT])

            with sp.Fori(0, B) as b:
                sp.wait_ge(s_pre, 25)
                sp.dma_start(X[:, :, :], x[ds(b, 1), :, :].rearrange("a (t p) d -> p (a t) d", p=P)).then_inc(m_x, 16)

                def moves(p, first, last):
                    g, U0 = b * NP + p, b * NU + p * UP
                    if not last:
                        wait_apart(sp, p_w, g + 2)
                        load_w_next(p)
                    if not first:
                        wait_apart(sp, s_pv, NT * U0)
                    place_v(1)
                    wait_apart(sp, p_wo[1], g + 1)
                    load_wo_next(1, p)
                    wait_apart(sp, p_wo[0], g + 1)
                    load_wo_next(0, p)
                    if last:
                        return
                    wait_apart(sp, d_qkv, NQ * (g + 1) + 4)
                    wait_apart(sp, s_sc, UT * (U0 + 2))
                    place_qk(0)
                    wait_apart(sp, s_sc, UT * (U0 + 4))
                    place_qk(1)
                    wait_apart(sp, d_qkv, NQ * (g + 2))
                    wait_apart(sp, s_pv, NT * (U0 + 2))
                    place_v(0)

                def load_w_next(p):
                    nxt = p + 2
                    load_w(nxt if isinstance(nxt, int) and nxt < NP else (nxt % NP if isinstance(nxt, int) else nxt))

                def load_wo_next(h, p):
                    nxt = p + 1
                    load_wo(h, nxt % NP if isinstance(nxt, int) else nxt)

                wait_apart(sp, d_qkv, NQ * (b * NP) + 4)
                place_qk(0)
                place_qk(1)
                wait_apart(sp, d_qkv, NQ * (b * NP) + NQ)
                place_v(0)
                wait_apart(sp, p_w, b * NP + 1)
                load_w(1)
                moves(0, True, False)
                with sp.Fori(1, NP - 2) as p:
                    moves(p, False, False)
                moves(NP - 2, False, False)
                moves(NP - 1, False, True)
                for i in range(NPT):
                    sp.wait_ge(m_scr[i], 64 * (16 // NPT))
                for h in range(2):
                    wait_apart(sp, m_qk[h], 96 * (b + 1) * NP)
                for l in range(2):
                    move(Mx[l], M_d[l, ds(b, 1)].rearrange("a p k n -> p (a k) n"), m_m)
                wait_apart(sp, s_sc, UT * NU * (b + 1))
                for l in range(2):
                    move(VWx[l], VW_d[l, ds(b, 1)].rearrange("a p n d -> p (a n) d"), m_vw)
                for r in range(2):
                    wait_apart(sp, d_fx, 2 * (2 * b + r + 1))
                    sp.dma_start(out[ds(b, 1), 512 * r:512 * r + 512, :].rearrange("a (t p) d -> p (a t) d", p=P),
                                 X[:, 4 * r:4 * r + 4, :]).then_inc(m_out, 16)
                wait_apart(sp, m_out, 32 * (b + 1))

        @block.gpsimd
        def _(pool):
            def split(raw, hi, lo, count):
                nc.gpsimd.tensor_copy(hi, raw).then_inc(p_wh, 1)
                pool.wait_ge(p_wh, count)
                return nc.gpsimd.tensor_tensor(lo, raw, hi.bitcast(F32), ALU.subtract)

            nc.gpsimd.memset(ident[:, :], 0.0).then_inc(p_id, 1)
            pool.wait_ge(p_id, 1)
            nc.gpsimd.affine_select(out=ident[:, :], in_=ident[:, :], compare_op=ALU.not_equal, fill=1.0,
                                    base=0, pattern=[[-1, P]], channel_multiplier=1).then_inc(p_id, 1)
            nc.gpsimd.memset(kblk, 0.0).then_inc(p_blk, 1)
            nc.gpsimd.memset(vblk, 0.0).then_inc(p_blk, 1)
            pool.wait_ge(m_w, 48)
            split(w_raw[:, :, :, :], w_s[0][:, :, :, :], w_s[1][:, :, :, :], 1).then_inc(p_w, 1)
            def load_chunk(c):
                if c < 8:
                    pool.dma_start(f_raw[:, c % 2, :], ff_w1[P * (c // 4):P * (c // 4 + 1), BANK * (c % 4):BANK * (c % 4 + 1)])\
                        .then_inc(m_f[c % 2], 16)
                else:
                    pool.dma_start(f_raw[:, c % 2, :].rearrange("p (f d) -> p f d", d=D),
                                   ff_w2[2 * P * (c - 8):2 * P * (c - 7), :].rearrange("(f p) d -> p f d", p=P)).then_inc(m_f[c % 2], 16)

            load_chunk(0)
            for c in range(FW_CHUNKS):
                if c + 1 < FW_CHUNKS:
                    if c >= 1:
                        pool.wait_ge(p_f, c)
                    load_chunk(c + 1)
                pool.wait_ge(m_f[c % 2], 16 * (c // 2 + 1))
                hi, lo = (W1[l][:, c // 4, BANK * (c % 4):BANK * (c % 4 + 1)] if c < 8 else
                          W2[l][:, 2 * (c - 8):2 * (c - 7), :].rearrange("p f d -> p (f d)") for l in range(2))
                split(f_raw[:, c % 2, :], hi, lo, 2 + c).then_inc(p_f, 1)
            NW0 = 1 + FW_CHUNKS

            with pool.Fori(0, B) as b:
                def add_bias(i):
                    pool.wait_ge(d_z, NT * (3 * b + i + 1))
                    if i == 0:
                        pool.wait_ge(m_cst, 16 * 10)
                    nc.gpsimd.tensor_tensor(X[:, :, :], X[:, :, :],
                                            bias_row[:, i:i + 1, :].to_broadcast([P, NT, D]), ALU.add).then_inc(p_xb, 1)

                def split_wo(h, p, count):
                    g = b * NP + p
                    pool.wait_ge(m_wo[h], 32 * (g + 1))
                    if not (isinstance(p, int) and p == 0):
                        wait_apart(pool, s_op, 2 * UP * g - 4 * (1 - h))
                    else:
                        wait_apart(pool, d_z, NT * (3 * b + 1))
                    split(wo_raw[h][:, :], wo_s[h][0][:, :], wo_s[h][1][:, :], count).then_inc(p_wo[h], 1)

                def split_w(p, count):
                    g = b * NP + p
                    pool.wait_ge(m_w, 48 * (g + 1))
                    wait_apart(pool, s_qkv, NQ * g)
                    split(w_raw[:, :, :, :], w_s[0][:, :, :, :], w_s[1][:, :, :, :], count).then_inc(p_w, 1)

                per_b = 3 * NP
                base = NW0 + b * per_b
                add_bias(0)
                split_wo(0, 0, base + 1)
                split_w(1, base + 2)
                split_wo(1, 0, base + 3)
                with pool.Fori(1, NP - 1) as p:
                    split_wo(0, p, base + 3 * p + 1)
                    split_w(p + 1, base + 3 * p + 2)
                    split_wo(1, p, base + 3 * p + 3)
                split_wo(0, NP - 1, base + 3 * (NP - 1) + 1)
                split_wo(1, NP - 1, base + 3 * (NP - 1) + 2)
                pool.wait_ge(m_w, 48 * ((b + 1) * NP + 1))
                wait_apart(pool, s_qkv, NQ * (b + 1) * NP)
                split(w_raw[:, :, :, :], w_s[0][:, :, :, :], w_s[1][:, :, :, :], base + 3 * NP).then_inc(p_w, 1)
                add_bias(1)
                for t in range(NT):
                    C = b * NT + t
                    pool.wait_ge(d_cr, C + 1)
                    e3 = E[t % 4].rearrange("p (h k) -> p h k", k=T)
                    nc.gpsimd.tensor_tensor(e3, e3, crec[:, t % 2, :].rearrange("p (h a) -> p h a", a=1)
                                            .to_broadcast([P, NH, T]), ALU.mult).then_inc(p_cn, 1)
                add_bias(2)

        @block.tensor
        def _(pe):
            mm = nc.tensor.matmul

            pe.wait_ge(p_id, 2)
            pe.wait_ge(m_cnd, 16)
            nc.tensor.transpose(MISC[:, 0:P], cnd[:, 0:P], ident[:, :])
            nc.tensor.transpose(MISC[0:DC - P, P:2 * P], cnd[:, P:DC], ident[:, :]).then_inc(s_pre, 1)
            pe.wait_ge(d_pre, 1)
            pe.wait_ge(m_kv, 64)
            for m, (wa, wb) in enumerate(((wk_a, wk_b), (wv_a, wv_b))):
                for q in range(2):
                    for n in range(4 * q, 4 * q + 4):
                        o = SC[m][:, n * P:(n + 1) * P]
                        mm(o, wa[:, n * P:(n + 1) * P], cndT[:, 0, :], start=True, stop=False)
                        last = mm(o, wb[:, n * P:(n + 1) * P], cndT[0:DC - P, 1, :], start=False, stop=True)
                    last.then_inc(s_pre, 1)
            pe.wait_ge(m_caq, 16)
            for i in range(4):
                bank = (TP[0], TP[1], PV, MISC)[i]
                for n in (2 * i, 2 * i + 1):
                    for k in range(KD):
                        c = (n % 2) * D + k * P
                        last = nc.tensor.transpose(bank[:, c:c + P], caq[:, k, n * P:(n + 1) * P], ident[:, :])
                last.then_inc(s_pre, 1)
            pe.wait_ge(d_pre, 9)
            for i in range(16):
                bank = SC[i // 2 % 2][:, BANK * (i % 2):BANK * (i % 2 + 1)]
                if i >= 4:
                    pe.wait_ge(d_pre, 10 + i - 4)
                if i == 8:
                    pe.wait_ge(m_cao, 16)
                for a in range(2):
                    o = bank[:, 256 * a:256 * a + 256]
                    if i < 8:
                        k, n = i // 4, 2 * (i % 4) + a
                        last = mm(o, wqT[:, n, k * P:(k + 1) * P], kblk[:, n, :, :], start=True, stop=True)
                    else:
                        last = mm(o, vblk[:, i - 8, a, :], X[:, i - 8, :], start=True, stop=True)
                last.then_inc(s_pre, 1)

            def transpose_h(L):
                for n in range(4):
                    r, k = n // 2, n % 2
                    pe.wait_ge(d_z, NT * L + 4 * r + 4)
                    for i in range(4):
                        last = nc.tensor.transpose(SC[r][:, k * BANK + i * P:k * BANK + (i + 1) * P],
                                                   z[:, 4 * r + i, k * P:(k + 1) * P], ident[:, :])
                    last.then_inc(s_tr, 1)

            with pe.Fori(0, B) as b:
                def project(n, bank):
                    kind, half = PROJ[n]
                    if kind == "v":
                        for i in range(4):
                            kt = 4 * half + i
                            for c, (l, r) in enumerate(TERMS):
                                for k in range(KD):
                                    last = mm(bank[:, i * P:(i + 1) * P], hT[l][:, k, kt * P:(kt + 1) * P],
                                              w_s[r][:, 2, k, :], start=(c == 0 and k == 0), stop=(c == 2 and k == KD - 1))
                    else:
                        m = "qk".index(kind)
                        for c, (l, r) in enumerate(TERMS):
                            for k in range(KD):
                                last = mm(bank[:, :], w_s[l][:, m, k, :], hT[r][:, k, half * BANK:(half + 1) * BANK],
                                          start=(c == 0 and k == 0), stop=(c == 2 and k == KD - 1))
                    last.then_inc(s_qkv, 1)

                def scores(tau, half):
                    h, qt = tau // 8 % 2, tau % 8
                    o = SC[tau % 2][:, half * BANK:(half + 1) * BANK]
                    for l in range(2):
                        last = mm(o, QKS[:, 3 * h, qt * P:(qt + 1) * P],
                                  QKS[:, 3 * h + 1 + l, half * BANK:(half + 1) * BANK], start=(l == 0), stop=(l == 1))
                    if half == 1:
                        last.then_inc(s_sc, 1)

                def attend(U, s, j):
                    h = s // 2
                    pe.wait_ge(d_pl, NT * U + j + 1)
                    for l in range(2):
                        last = mm(PV[:, :], VS[h][:, j, :], PT[l][:, j % NPT, :], start=(j == 0 and l == 0),
                                  stop=(j == NT - 1 and l == 1))
                    last.then_inc(s_pv, 1)

                def project_out(U, h, k):
                    for i in (2 * k, 2 * k + 1):
                        for c, (l, r) in enumerate(TERMS):
                            last = mm(MISC[:, D * (i % 2):D * (i % 2) + D], OT[l][:, i * P:(i + 1) * P],
                                      wo_s[h][r][:, :], start=(c == 0), stop=(c == 2))
                    last.then_inc(s_op, 1)

                transpose_h(3 * b)
                pe.wait_ge(d_hl, 4 * (3 * b) + 4)
                pe.wait_ge(p_w, b * NP + 1)
                for n in range(NQ):
                    if n >= 2:
                        pe.wait_ge(d_qkv, NQ * b * NP + n - 1)
                    project(n, (MISC, PV)[n % 2])
                pe.wait_ge(m_qk[0], 96 * (b * NP + 1))
                for tau in range(5):
                    if tau >= 2:
                        pe.wait_ge(a_exp, UT * NU * b + tau - 1)
                    scores(tau, 0)
                    scores(tau, 1)

                def pair(p, first, last):
                    g, U0 = b * NP + p, b * NU + p * UP
                    for s in range(UP):
                        U = U0 + s
                        for j in range(NT):
                            if j == 0:
                                pe.wait_ge(a_exp, UT * U + UT)
                            if not (first and s == 0 and j < 2):
                                pe.wait_ge(d_pl, NT * U + j - 1)
                            for i in range(UT):
                                tr = nc.tensor.transpose(TP[j % 2][:, i * P:(i + 1) * P],
                                                         PR[:, s % 2, i, j * P:(j + 1) * P], ident[:, :])
                            tr.then_inc(s_pt, 1)
                            tau = UT * s + 5 + j // 2
                            if not (last and tau >= 16):
                                if j % 2 == 0:
                                    pe.wait_ge(a_exp, UT * U0 + tau - 1)
                                    if tau == 8:
                                        pe.wait_ge(m_qk[1], 96 * (g + 1))
                                    if tau == 16:
                                        pe.wait_ge(m_qk[0], 96 * (g + 2))
                                scores(tau, j % 2)
                            if j < 2 and not (first and s == 0):
                                attend(U - 1, (s - 1) % UP, j + 6)
                            if j == 3:
                                if s == 0:
                                    pe.wait_ge(m_v[0], 16 * (g + 1))
                                if s == 2:
                                    pe.wait_ge(m_v[1], 16 * (g + 1))
                                if not (first and s == 0):
                                    pe.wait_ge(d_ol, U)
                                attend(U, s, 0)
                            if j >= 3:
                                attend(U, s, j - 2)
                            if j in (0, 2) and s < 3 and not last:
                                n = 2 * s + j // 2
                                if n == 0:
                                    pe.wait_ge(p_w, g + 2)
                                if j == 2 or (first and s < 2):
                                    pe.wait_ge(d_qkv, NQ * (g + 1) + n)
                                else:
                                    pe.wait_ge(d_x, 2 * U - 2)
                                project(n, MISC)
                            if j in (4, 6) and not (first and s == 0):
                                if j == 4:
                                    pe.wait_ge(d_ol, U)
                                    if s % 2 == 1:
                                        pe.wait_ge(p_wo[s // 2], g + 1)
                                    if s < 3 and not last:
                                        pe.wait_ge(d_qkv, NQ * (g + 1) + 2 * s + 2)
                                    elif not (first and s == 1):
                                        pe.wait_ge(d_x, 2 * U - 2)
                                else:
                                    pe.wait_ge(d_x, 2 * U - 1)
                                project_out(U - 1, (s - 1) % UP // 2, (j - 4) // 2)

                pair(0, True, False)
                with pe.Fori(1, NP - 1) as p:
                    pair(p, False, False)
                pair(NP - 1, False, True)
                UE = (b + 1) * NU
                attend(UE - 1, 3, 6)
                attend(UE - 1, 3, 7)
                pe.wait_ge(d_ol, UE)
                for k in range(2):
                    pe.wait_ge(d_x, 2 * UE - 2 + k)
                    project_out(UE - 1, 1, k)

                transpose_h(3 * b + 1)
                pe.wait_ge(d_hl, 4 * (3 * b + 1) + 4)
                pe.wait_ge(m_m, 32 * (b + 1))
                for t in range(NT + 3):
                    C = b * NT + t
                    if t < NT:
                        if t >= 2:
                            pe.wait_ge(d_cs, C - 1)
                        for half in range(2):
                            for c, (l, r) in enumerate(TERMS):
                                for k in range(KD):
                                    last = mm(SC[t % 2][:, half * BANK:(half + 1) * BANK], hT[l][:, k, t * P:(t + 1) * P],
                                              Mx[r][:, k, half * BANK:(half + 1) * BANK],
                                              start=(c == 0 and k == 0), stop=(c == 2 and k == KD - 1))
                        last.then_inc(s_cs, 1)
                    if 2 <= t < NT + 2:
                        pe.wait_ge(p_cn, C - 1)
                        for k in range(2):
                            if t > 2:
                                pe.wait_ge(d_cl, 2 * (C - 2) + k - 1)
                            for i in range(4):
                                last = nc.tensor.transpose(TP[k][:, i * P:(i + 1) * P],
                                                           E[(t - 2) % 4][:, (4 * k + i) * P:(4 * k + i + 1) * P], ident[:, :])
                            last.then_inc(s_ct, 1)
                    if t >= 3:
                        if t == 3:
                            pe.wait_ge(m_vw, 32 * (b + 1))
                        if t >= 5:
                            pe.wait_ge(d_cx, C - 4)
                        pe.wait_ge(d_cl, 2 * (C - 3) + 2)
                        for n in range(NP):
                            for c, (l, r) in enumerate(TERMS):
                                last = mm((PV, MISC)[(t - 3) % 2][:, 0:D],
                                          PT[l][:, (2 * (t - 3) + n // 4) % NPT, (n % 4) * P:(n % 4 + 1) * P], VWx[r][:, n, :],
                                          start=(n == 0 and c == 0), stop=(n == NP - 1 and c == 2))
                        last.then_inc(s_co, 1)

                transpose_h(3 * b + 2)
                pe.wait_ge(d_hl, 4 * (3 * b + 2) + 4)
                pe.wait_ge(p_f, FW_CHUNKS)

                def ff_down(F, r, f):
                    pe.wait_ge(d_ul, F + 1)
                    for i in range(4):
                        bank = ((TP[0], TP[1]), (PV, MISC))[r][i // 2]
                        for c, (l, m) in enumerate(TERMS):
                            last = mm(bank[:, D * (i % 2):D * (i % 2) + D], PT[l][:, f % NPT, i * P:(i + 1) * P],
                                      W2[m][:, f, :], start=(f == 0 and c == 0 and i % 2 == 0),
                                      stop=(f == NF - 1 and c == 2), skip_group_check=True)
                    last.then_inc(s_w2, 1)

                for r in range(2):
                    for f in range(NF + 1):
                        F = b * 2 * NF + r * NF + f
                        if f < NF:
                            if r or f >= 2:
                                pe.wait_ge(d_u, F - 1)
                            for part, col in enumerate((FF + f * P, f * P)):
                                for c, (l, m) in enumerate(TERMS):
                                    for k in range(KD):
                                        last = mm(SC[f % 2][:, part * BANK:(part + 1) * BANK], W1[l][:, k, col:col + P],
                                                  hT[m][:, k, r * BANK:(r + 1) * BANK],
                                                  start=(c == 0 and k == 0), stop=(c == 2 and k == KD - 1))
                            last.then_inc(s_ff, 1)
                        if f >= 1:
                            ff_down(F - 1, r, f - 1)

        @block.scalar
        def _(act):
            for i in range(16):
                bank = SC[i // 2 % 2][:, BANK * (i % 2):BANK * (i % 2 + 1)]
                act.wait_ge(s_pre, 10 + i)
                if i >= NPT:
                    act.wait_ge(m_scr[i % NPT], 64 * (i // NPT))
                nc.scalar.copy(PT[0][:, i % NPT, :], bank).then_inc(a_pre, 1)

            for i in range(NPT):
                act.wait_ge(m_scr[i], 64 * (16 // NPT))
            with act.Fori(0, B) as b:
                def norm(L):
                    act.wait_ge(d_mv, NT * (L + 1))
                    nc.scalar.activation(sd[:, :], mv[:, :, 1], ACT.Sqrt, bias=EPS).then_inc(a_sd, 1)
                    for n in range(4):
                        r, k = n // 2, n % 2
                        act.wait_ge(d_h, 4 * L + n + 1)
                        nc.scalar.copy(hT[0][:, k, r * BANK:(r + 1) * BANK], h32[:, k, r * BANK:(r + 1) * BANK]).then_inc(a_hh, 1)

                def split_qkv(g, n, bank):
                    kind, half = PROJ[n]
                    act.wait_ge(s_qkv, NQ * g + n + 1)
                    if kind == "v":
                        nc.scalar.copy(VT[:, :, 4 * half:4 * half + 4, 0:DH].rearrange("p h k d -> p k h d"),
                                       bank[:, :].rearrange("p (k h d) -> p k h d", k=4, h=2)).then_inc(a_qkv, 1)
                    else:
                        nc.scalar.mul(QKT[:, 2 * "qk".index(kind), half * BANK:(half + 1) * BANK], bank[:, :],
                                      SCALE if kind == "q" else 1.0).then_inc(a_qkv, 1)

                def exp(U0, tau):
                    u = tau // UT
                    act.wait_ge(d_max, UT * U0 + tau + 1)
                    nc.scalar.activation(PR[:, u % 2, tau % UT, :], SC[tau % 2][:, :], ACT.Exp,
                                         bias=nmax[:, tau % 4:tau % 4 + 1],
                                         accum_out=den[:, u % 2, tau % UT:tau % UT + 1]).then_inc(a_exp, 1)

                def split_out(U, first):
                    act.wait_ge(s_pv, NT * U + NT)
                    if not first:
                        act.wait_ge(s_op, 2 * U)
                    nc.scalar.copy(OT[0][:, :], PV[:, :]).then_inc(a_oh, 1)

                norm(3 * b)
                for n in range(NQ):
                    split_qkv(b * NP, n, (MISC, PV)[n % 2])
                for tau in range(4):
                    exp(b * NU, tau)

                def pair(p, first, last):
                    g, U0 = b * NP + p, b * NU + p * UP
                    for s in range(UP):
                        U = U0 + s
                        for j in range(NT):
                            tau = UT * s + 4 + j // 2
                            if j % 2 == 0 and not (last and tau >= 16):
                                if j == 0 and not (first and s == 0):
                                    act.wait_ge(s_pt, NT * U)
                                if j == 0 and not (first and s == 0):
                                    act.wait_ge(d_rd, U)
                                exp(U0, tau)
                            act.wait_ge(s_pt, NT * U + j + 1)
                            if not (first and s == 0 and j < NPT):
                                act.wait_ge(s_pv, NT * U + j - NPT + 1)
                            nc.scalar.copy(PT[0][:, j % NPT, :], TP[j % 2][:, :]).then_inc(a_ph, 1)
                            if j == 2 and not (first and s == 0):
                                split_out(U - 1, first and s == 1)
                            if j in (1, 3) and s < 3 and not last:
                                n = 2 * s + j // 2
                                if n == 0:
                                    act.wait_ge(m_qk[1], 96 * (g + 1))
                                    act.wait_ge(m_qk[0], 96 * (g + 1))
                                if n == 4:
                                    act.wait_ge(m_v[0], 16 * (g + 1))
                                    act.wait_ge(m_v[1], 16 * (g + 1))
                                split_qkv(g + 1, n, MISC)

                pair(0, True, False)
                with act.Fori(1, NP - 1) as p:
                    pair(p, False, False)
                pair(NP - 1, False, True)
                split_out((b + 1) * NU - 1, False)

                norm(3 * b + 1)
                for t in range(NT + 2):
                    C = b * NT + t
                    if t < NT:
                        act.wait_ge(d_cs, C + 1)
                        nc.scalar.activation(E[t % 4], E[t % 4], ACT.Exp).then_inc(a_ce, 1)
                    if t >= 2:
                        for k in range(2):
                            act.wait_ge(s_ct, 2 * (C - 2) + k + 1)
                            if t >= 4:
                                act.wait_ge(s_co, C - 3)
                            nc.scalar.copy(PT[0][:, (2 * (t - 2) + k) % NPT, :], TP[k][:, :]).then_inc(a_ch, 1)

                norm(3 * b + 2)
                for r in range(2):
                    for f in range(NF + 1):
                        F = b * 2 * NF + r * NF + f
                        if f < NF:
                            act.wait_ge(s_ff, F + 1)
                            if r or f >= 2:
                                act.wait_ge(d_u, F - 1)
                            nc.scalar.activation(G[f % 2], SC[f % 2][:, 0:BANK], ACT.Gelu,
                                                 bias=b1[:, NF + f:NF + f + 1]).then_inc(a_g, 1)
                        if f >= 1:
                            act.wait_ge(d_u, F)
                            if r or f - 1 >= NPT:
                                act.wait_ge(s_w2, F - NPT)
                            nc.scalar.copy(PT[0][:, (f - 1) % NPT, :], U32[(f - 1) % 2]).then_inc(a_uh, 1)

        @block.vector
        def _(dve):
            V = nc.vector
            sub = ALU.subtract

            dve.wait_ge(s_pre, 1)
            V.tensor_copy(cndT[:, 0, :], MISC[:, 0:P])
            V.tensor_copy(cndT[0:DC - P, 1, :], MISC[0:DC - P, P:2 * P]).then_inc(d_pre, 1)
            dve.wait_ge(p_blk, 2)
            for m, blk in enumerate((kblk, vblk)):
                for q in range(2):
                    dve.wait_ge(s_pre, 2 + 2 * m + q)
                    for h in range(2):
                        rows = slice(64 * h, 64 * h + 64)
                        src = SC[m][rows, q * BANK:(q + 1) * BANK].rearrange("p (n b c) -> p n b c", n=4, b=B)
                        last = V.tensor_scalar(blk[rows, 4 * q:4 * q + 4, :, 64 * h:64 * h + 64], src,
                                               (SCALE, 1.0)[m], None, ALU.mult)
                    last.then_inc(d_pre, 1)
            for i in range(4):
                dve.wait_ge(s_pre, 6 + i)
                V.tensor_copy(wqT[:, 2 * i:2 * i + 2, :].rearrange("p n c -> p (n c)"),
                              (TP[0], TP[1], PV, MISC)[i][:, :]).then_inc(d_pre, 1)
            for i in range(16):
                bank = SC[i // 2 % 2][:, BANK * (i % 2):BANK * (i % 2 + 1)]
                dve.wait_ge(a_pre, i + 1)
                V.tensor_tensor(PT[1][:, i % NPT, :], bank, PT[0][:, i % NPT, :].bitcast(F32), sub).then_inc(d_pre, 1)

            with dve.Fori(0, B) as b:
                def norm(L, i):
                    for t in range(NT):
                        V.bn_stats(st[:, t, :], X[:, t, :]).then_inc(d_st, 1)
                    wait_apart(dve, d_st, NT * (L + 1))
                    for t in range(NT):
                        V.bn_aggr(mv[:, t, :], st[:, t, :]).then_inc(d_mv, 1)
                    dve.wait_ge(a_sd, L + 1)
                    V.reciprocal(rs[:, :], sd[:, :]).then_inc(d_rs, 1)
                    dve.wait_ge(d_rs, L + 1)
                    for t in range(NT):
                        V.tensor_scalar(z[:, t, :], X[:, t, :], mv[:, t, 0:1], rs[:, t:t + 1], sub, ALU.mult).then_inc(d_z, 1)
                    for n in range(5):
                        r, k = n // 2, n % 2
                        if n < 4:
                            dve.wait_ge(s_tr, 4 * L + n + 1)
                            V.tensor_scalar(h32[:, k, r * BANK:(r + 1) * BANK], SC[r][:, k * BANK:(k + 1) * BANK],
                                            gb[:, i, 0, k:k + 1], gb[:, i, 1, k:k + 1], ALU.mult, ALU.add).then_inc(d_h, 1)
                        if n >= 1:
                            r, k = (n - 1) // 2, (n - 1) % 2
                            dve.wait_ge(a_hh, 4 * L + n)
                            V.tensor_tensor(hT[1][:, k, r * BANK:(r + 1) * BANK], h32[:, k, r * BANK:(r + 1) * BANK],
                                            hT[0][:, k, r * BANK:(r + 1) * BANK].bitcast(F32), sub).then_inc(d_hl, 1)

                def split_qkv(g, n, bank):
                    kind, half = PROJ[n]
                    dve.wait_ge(a_qkv, NQ * g + n + 1)
                    if kind == "v":
                        V.tensor_tensor(VT[:, :, 4 * half:4 * half + 4, DH:P].rearrange("p h k d -> p k h d"),
                                        bank[:, :].rearrange("p (k h d) -> p k h d", k=4, h=2),
                                        VT[:, :, 4 * half:4 * half + 4, 0:DH].rearrange("p h k d -> p k h d").bitcast(F32),
                                        sub).then_inc(d_qkv, 1)
                    else:
                        m, cols = 2 * "qk".index(kind), slice(half * BANK, (half + 1) * BANK)
                        V.scalar_tensor_tensor(QKT[:, m + 1, cols], bank[:, :], SCALE if kind == "q" else 1.0,
                                               QKT[:, m, cols].bitcast(F32), ALU.mult, sub).then_inc(d_qkv, 1)

                def rowmax(U0, tau, fresh):
                    dve.wait_ge(s_sc, UT * U0 + tau + 1)
                    if not fresh:
                        dve.wait_ge(a_exp, UT * U0 + tau - 3)
                    V.tensor_reduce(nmax[:, tau % 4:tau % 4 + 1], SC[tau % 2][:, :], AX, ALU.max, negate=True).then_inc(d_max, 1)

                def split_out(U):
                    dve.wait_ge(a_oh, U + 1)
                    V.tensor_tensor(OT[1][:, :], PV[:, :], OT[0][:, :].bitcast(F32), sub).then_inc(d_ol, 1)

                def add_out(U, s, k):
                    dve.wait_ge(s_op, 2 * U + k + 1)
                    for i in (2 * k, 2 * k + 1):
                        t = UT * (s % 2) + i
                        last = V.scalar_tensor_tensor(X[:, t, :], MISC[:, D * (i % 2):D * (i % 2) + D],
                                                      rden[:, s % 2, i:i + 1], X[:, t, :], ALU.mult, ALU.add)
                    last.then_inc(d_x, 1)

                dve.wait_ge(m_x, 16 * (b + 1))
                dve.wait_ge(m_cst, 160)
                norm(3 * b, 0)
                for n in range(NQ):
                    split_qkv(b * NP, n, (MISC, PV)[n % 2])
                for tau in range(5):
                    rowmax(b * NU, tau, tau < 4)
                dve.wait_ge(p_xb, 3 * b + 1)

                def pair(p, first, last):
                    g, U0 = b * NP + p, b * NU + p * UP
                    for s in range(UP):
                        U = U0 + s
                        for j in range(NT):
                            dve.wait_ge(a_ph, NT * U + j + 1)
                            V.tensor_tensor(PT[1][:, j % NPT, :], TP[j % 2][:, :], PT[0][:, j % NPT, :].bitcast(F32),
                                            sub).then_inc(d_pl, 1)
                            tau = UT * s + 5 + j // 2
                            if j % 2 == 1 and not (last and tau >= 16):
                                rowmax(U0, tau, False)
                            if j == 1:
                                dve.wait_ge(a_exp, UT * U + UT)
                                if not (first and s < 2):
                                    dve.wait_ge(d_x, 2 * U - 2)
                                V.reciprocal(rden[:, s % 2, :], den[:, s % 2, :]).then_inc(d_rd, 1)
                            if j == 2 and not (first and s == 0):
                                split_out(U - 1)
                            if j in (1, 3) and s < 3 and not last:
                                split_qkv(g + 1, 2 * s + j // 2, MISC)
                            if j in (5, 7) and not (first and s == 0):
                                add_out(U - 1, (s - 1) % UP, (j - 5) // 2)

                pair(0, True, False)
                with dve.Fori(1, NP - 1) as p:
                    pair(p, False, False)
                pair(NP - 1, False, True)
                split_out((b + 1) * NU - 1)
                for k in range(2):
                    add_out((b + 1) * NU - 1, 3, k)
                dve.wait_ge(d_x, 2 * NU * (b + 1))

                norm(3 * b + 1, 1)
                dve.wait_ge(p_xb, 3 * b + 2)
                for t in range(NT + 3):
                    C = b * NT + t
                    if t < NT:
                        ps3 = SC[t % 2][:, :].rearrange("p (h k) -> p h k", k=T)
                        bc = lambda v: v[:, t % 2, :].rearrange("p (h a) -> p h a", a=1).to_broadcast([P, NH, T])
                        dve.wait_ge(s_cs, C + 1)
                        V.tensor_reduce(cmax[:, t % 2, :], ps3, AX, ALU.max).then_inc(d_cm, 1)
                        dve.wait_ge(d_cm, C + 1)
                        if t >= 4:
                            dve.wait_ge(s_ct, 2 * (C - 3))
                        V.tensor_tensor(E[t % 4].rearrange("p (h k) -> p h k", k=T), ps3, bc(cmax), sub).then_inc(d_cs, 1)
                    if 1 <= t < NT + 1:
                        dve.wait_ge(a_ce, C)
                        V.tensor_reduce(csum[:, (t - 1) % 2, :], E[(t - 1) % 4].rearrange("p (h k) -> p h k", k=T),
                                        AX, ALU.add).then_inc(d_csum, 1)
                        dve.wait_ge(d_csum, C)
                        if t >= 3:
                            dve.wait_ge(p_cn, C - 2)
                        V.reciprocal(crec[:, (t - 1) % 2, :], csum[:, (t - 1) % 2, :]).then_inc(d_cr, 1)
                    if 2 <= t < NT + 2:
                        for k in range(2):
                            dve.wait_ge(a_ch, 2 * (C - 2) + k + 1)
                            slot = (2 * (t - 2) + k) % NPT
                            V.tensor_tensor(PT[1][:, slot, :], TP[k][:, :], PT[0][:, slot, :].bitcast(F32), sub).then_inc(d_cl, 1)
                    if t >= 3:
                        dve.wait_ge(s_co, C - 2)
                        V.tensor_tensor(X[:, t - 3, :], (PV, MISC)[(t - 3) % 2][:, 0:D], X[:, t - 3, :], ALU.add).then_inc(d_cx, 1)
                dve.wait_ge(d_cx, NT * (b + 1))

                norm(3 * b + 2, 2)
                dve.wait_ge(p_xb, 3 * b + 3)
                for r in range(2):
                    for f in range(NF + 1):
                        F = b * 2 * NF + r * NF + f
                        if f < NF:
                            dve.wait_ge(a_g, F + 1)
                            if r or f >= 2:
                                dve.wait_ge(a_uh, F - 1)
                            V.scalar_tensor_tensor(U32[f % 2], SC[f % 2][:, BANK:2 * BANK], b1[:, f:f + 1], G[f % 2],
                                                   ALU.add, ALU.mult).then_inc(d_u, 1)
                        if f >= 1:
                            dve.wait_ge(a_uh, F)
                            V.tensor_tensor(PT[1][:, (f - 1) % NPT, :], U32[(f - 1) % 2],
                                            PT[0][:, (f - 1) % NPT, :].bitcast(F32), sub).then_inc(d_ul, 1)
                    dve.wait_ge(s_w2, NF * (2 * b + r + 1))
                    for i in range(2):
                        xs = X[:, 4 * r + 2 * i:4 * r + 2 * i + 2, :].rearrange("p t d -> p (t d)")
                        V.tensor_tensor(xs, ((TP[0], TP[1]), (PV, MISC))[r][i][:, :], xs, ALU.add).then_inc(d_fx, 1)


_INS = ['x', 'ctx_768'] + ['L0_xattn_' + n for n in (
    'ln1_g', 'ln1_b', 'ln2_g', 'ln2_b', 'ln3_g', 'ln3_b', 'sa_wq', 'sa_wk', 'sa_wv', 'sa_wo', 'sa_bo',
    'ca_wq', 'ca_wk', 'ca_wv', 'ca_wo', 'ca_bo', 'ff_w1', 'ff_b1', 'ff_w2', 'ff_b2')]
_OUTS = [((2, 1024, 256), 'float32')]


def kernel(**inputs):
    import numpy as _np
    import concourse.bacc as _bacc
    from concourse import mybir as _mybir
    from concourse.bass_utils import run_bass_kernel_spmd as _run

    nc = _bacc.Bacc("TRN2", target_bir_lowering=False, num_devices=1)
    arrays, args = {}, []
    for name in _INS:
        a = _np.ascontiguousarray(inputs[name])
        arrays[f"in_{name}_dram"] = a
        args.append(nc.dram_tensor(f"in_{name}_dram", a.shape, _mybir.dt.from_np(a.dtype), kind="ExternalInput").ap())
    for i, (shape, dtype) in enumerate(_OUTS):
        dt = _mybir.dt.from_np(_np.dtype(dtype))
        args.append(nc.dram_tensor(f"out_{i}_dram", shape, dt, kind="ExternalOutput").ap())
    build_block(nc, *args)
    r = _run(nc, [arrays], core_ids=[0])
    got = tuple(r.results[0][f"out_{i}_dram"] for i in range(len(_OUTS)))
    return got[0]
```

```python
from contextlib import ExitStack

import concourse.bass as bass
from concourse import mybir

F32 = mybir.dt.float32
F32R = mybir.dt.float32r
ALU = mybir.AluOpType
ACT = mybir.ActivationFunctionType
AX = mybir.AxisListType.X
ds = bass.ds

P = 128
BANK = 512
EPS = 1e-5


def build_block(nc, x, cond, ln1_g, ln1_b, ln2_g, ln2_b, ln3_g, ln3_b, sa_wq, sa_wk, sa_wv, sa_wo, sa_bo,
                ca_wq, ca_wk, ca_wv, ca_wo, ca_bo, ff_w1, ff_b1, ff_w2, ff_b2, out):
    B, S, D = x.shape
    T, DC = cond.shape[1:]
    DA = sa_wq.shape[1]
    FF = ff_w2.shape[0]
    DH = 64
    NH = DA // DH
    NP = NH // 2
    NT = S // P
    KD = D // P
    NF = FF // P
    UP = 4
    NU = NP * UP
    UT = 4
    NPT = 4
    SCALE = float(DH) ** -0.5
    assert (B, S, D, T, DC, DA, FF) == (2, 1024, 256, 64, 192, 1024, 1024)

    with ExitStack() as ctx:
        def sb(name, shape, dt=F32):
            return ctx.enter_context(nc.sbuf_tensor(name, shape, dt))

        def sem(name):
            return ctx.enter_context(nc.semaphore(name))

        X = sb("X", [P, NT, D])
        hT = [sb("hT_hi", [P, KD, S], F32R), sb("hT_lo", [P, KD, S], F32R)]
        PR = sb("PR", [P, 2, UT, S])
        PT = [sb("PT_hi", [P, NPT, BANK], F32R), sb("PT_lo", [P, NPT, BANK], F32R)]
        QKT = sb("QKT", [P, 4, S], F32R)
        QKS = sb("QKS", [P, 6, S], F32R)
        VS = [sb(f"VS{h}", [P, NT, P], F32R) for h in range(2)]
        VX = sb("VX", [P, NT, P], F32R)
        WV_hi = sb("WV_hi", [P, KD, DA], F32R)
        OT = [sb("OT_hi", [P, BANK], F32R), sb("OT_lo", [P, BANK], F32R)]
        w_raw = sb("w_raw", [P, 2, KD, P])
        w_s = [sb("w_hi", [P, 2, KD, P], F32R), sb("w_lo", [P, 2, KD, P], F32R)]
        wo_raw = [sb(f"wo_raw{h}", [P, D]) for h in range(2)]
        wo_s = [[sb(f"wo_hi{h}", [P, D], F32R), sb(f"wo_lo{h}", [P, D], F32R)] for h in range(2)]
        W1 = [sb("W1_hi", [P, KD, 2 * FF], F32R), sb("W1_lo", [P, KD, 2 * FF], F32R)]
        W2 = [sb("W2_hi", [P, NF, D], F32R), sb("W2_lo", [P, NF, D], F32R)]
        ident = sb("ident", [P, P])
        bias_row = sb("bias_row", [P, 3, D])
        gb = sb("gb", [P, 3, 2, KD])
        b1 = sb("b1", [P, 2 * NF])
        f_raw = sb("f_raw", [P, 2, BANK])
        cnd = sb("cnd", [P, DC])
        cndT = sb("cndT", [P, 2, P])
        st = sb("st", [P, NT, 6])
        mv = sb("mv", [P, NT, 2])
        sd = sb("sd", [P, NT])
        rs = sb("rs", [P, NT])
        nmax = sb("nmax", [P, 4])
        den = sb("den", [P, 2, UT])
        rden = sb("rden", [P, 2, UT])
        cmax = sb("cmax", [P, 2, NH])
        csum = sb("csum", [P, 2, NH])
        crec = sb("crec", [P, 2, NH])

        M_d = nc.dram_tensor("scratch_m", [2, B, P, KD, DA], F32, kind="Internal").ap()
        VW_d = nc.dram_tensor("scratch_vw", [2, B, P, NP, D], F32, kind="Internal").ap()

        V_d = nc.dram_tensor("scratch_v", [NH, P, NT, P], F32, kind="Internal").ap()

        SC = [ctx.enter_context(nc.psum_tensor(f"SC{i}", [P, 2 * BANK], F32)) for i in range(2)]
        TP = [ctx.enter_context(nc.psum_tensor(f"TP{i}", [P, BANK], F32)) for i in range(2)]
        PV = ctx.enter_context(nc.psum_tensor("PV", [P, BANK], F32))
        MISC = ctx.enter_context(nc.psum_tensor("MISC", [P, BANK], F32))

        prf = PR[:, :, :, :].rearrange("p a b n -> p (a b) n")
        z = PR[:, 0, 0:2, :].rearrange("p a n -> p (a n)").rearrange("p (t d) -> p t d", d=D)
        h32 = PR[:, 0, 2:4, :]
        wk_a, wk_b, wv_a, wv_b = prf[:, 0, :], prf[0:DC - P, 1, :], prf[:, 2, :], prf[0:DC - P, 3, :]
        kblk = prf[:, 4:6, :].rearrange("p a n -> p (a n)").rearrange("p (n b c) -> p n b c", n=NP, b=B)
        vblk = prf[:, 6:8, :].rearrange("p a n -> p (a n)").rearrange("p (n b c) -> p n b c", n=NP, b=B)
        caq = prf[:, 0:2, :]
        wqT = prf[:, 2:4, :].rearrange("p a n -> p (a n)").rearrange("p (n c) -> p n c", c=D)
        E = [PR[:, 1, i, :] for i in range(4)]
        G = [PR[:, 0, i, 0:BANK] for i in range(2)]
        U32 = [PR[:, 0, 2 + i, 0:BANK] for i in range(2)]
        WV = [WV_hi, QKS[:, 4:6, :]]
        vstage = [VS[0][:, :, :], VS[1][:, :, :], VX[:, :, :], QKS[:, 3, :].rearrange("p (k c) -> p k c", c=P)]
        NV = 2 * NT
        Mx = [QKT[:, 0:2, :], QKT[:, 2:4, :]]
        vwf = QKS[:, 0:4, :].rearrange("p a n -> p (a n)").rearrange("p (l n d) -> p l n d", l=2, d=D)
        VWx = [vwf[:, 0], vwf[:, 1]]

        m_x = sem("m_x"); m_out = sem("m_out"); m_cst = sem("m_cst"); m_cnd = sem("m_cnd")
        m_kv = sem("m_kv"); m_caq = sem("m_caq"); m_cao = sem("m_cao"); m_scr = [sem(f"m_scr{i}") for i in range(4)]
        m_w = sem("m_w"); m_wo = [sem("m_wo0"), sem("m_wo1")]; m_f = [sem("m_f0"), sem("m_f1")]
        m_qk = [sem("m_qk0"), sem("m_qk1")]; m_v = [sem("m_v0"), sem("m_v1")]
        m_m = sem("m_m"); m_vw = sem("m_vw")
        waited = sem("waited")
        p_id = sem("p_id"); p_blk = sem("p_blk")
        p_w = sem("p_w"); p_wo = [sem("p_wo0"), sem("p_wo1")]; p_f = sem("p_f"); p_wh = sem("p_wh")
        p_xb = sem("p_xb"); p_cn = sem("p_cn")
        s_pre = sem("s_pre"); d_pre = sem("d_pre"); a_pre = sem("a_pre")
        d_st = sem("d_st"); d_mv = sem("d_mv"); a_sd = sem("a_sd"); d_rs = sem("d_rs"); d_z = sem("d_z")
        s_tr = sem("s_tr"); d_h = sem("d_h"); a_hh = sem("a_hh"); d_hl = sem("d_hl")
        s_sc = sem("s_sc"); d_max = sem("d_max"); a_exp = sem("a_exp"); d_rd = sem("d_rd")
        s_pt = sem("s_pt"); a_ph = sem("a_ph"); d_pl = sem("d_pl"); s_pv = sem("s_pv")
        a_oh = sem("a_oh"); d_ol = sem("d_ol"); s_op = sem("s_op"); d_x = sem("d_x")
        s_qkv = sem("s_qkv"); a_qkv = sem("a_qkv"); d_qkv = sem("d_qkv")
        p_wv = sem("p_wv"); s_v = sem("s_v"); a_v = sem("a_v"); d_v = sem("d_v"); m_vst = [sem(f"m_vst{i}") for i in range(4)]
        s_cs = sem("s_cs"); d_cm = sem("d_cm"); d_cs = sem("d_cs"); a_ce = sem("a_ce")
        d_csum = sem("d_csum"); d_cr = sem("d_cr"); s_ct = sem("s_ct"); a_ch = sem("a_ch"); d_cl = sem("d_cl")
        s_co = sem("s_co"); d_cx = sem("d_cx")
        s_ff = sem("s_ff"); a_g = sem("a_g"); d_u = sem("d_u"); a_uh = sem("a_uh"); d_ul = sem("d_ul")
        s_w2 = sem("s_w2"); d_fx = sem("d_fx")

        TERMS = [(0, 0), (0, 1), (1, 0)]

        PROJ = [("q", 0), ("k", 0), ("k", 1), ("q", 1)]
        NQ = len(PROJ)
        CHUNKS = 16

        def wait_apart(eng, signal, value):
            eng.wait_ge(signal, value)
            eng.sem_inc(waited, 1)

        block = ctx.enter_context(nc.Block())

        @block.sync
        def _(sp):
            def move(to, of, signal):
                sp.dma_start(to.bitcast(F32), of.bitcast(F32)).then_inc(signal, 16)

            def load_w(p):
                for m, w in enumerate((sa_wq, sa_wk)):
                    sp.dma_start(w_raw[:, m, :, :], w.rearrange("(k p) n -> p k n", p=P)[:, :, ds(p * P, P)])\
                      .then_inc(m_w, 16)

            def load_wo(h, p):
                for half in range(2):
                    sp.dma_start(wo_raw[h][64 * half:64 * half + 64, :], sa_wo[ds(p * P + 64 * h, 64), :])\
                      .then_inc(m_wo[h], 16)

            def place_qk(h):
                r = slice(64 * h, 64 * h + 64)
                for slot, (top, bottom) in enumerate(((0, 1), (2, 2), (3, 3))):
                    move(QKS[0:64, 3 * h + slot, :], QKT[r, top, :], m_qk[h])
                    move(QKS[64:128, 3 * h + slot, :], QKT[r, bottom, :], m_qk[h])

            def load_v(h, p):
                move(VS[h][:, :, :], V_d[ds(2 * p + h, 1)].rearrange("a p k c -> p (a k) c"), m_v[h])

            cw = lambda w: (w[0:P, :], w[P:DC, :])
            sp.dma_start(cnd[:, :], cond.rearrange("b t c -> (b t) c")).then_inc(m_cnd, 16)
            for dst, src in ((wk_a, cw(ca_wk)[0]), (wk_b, cw(ca_wk)[1]), (wv_a, cw(ca_wv)[0]), (wv_b, cw(ca_wv)[1])):
                sp.dma_start(dst, src).then_inc(m_kv, 16)
            sp.dma_start(X[:, :, :], ca_wo.rearrange("(n p) d -> p n d", p=P)).then_inc(m_cao, 16)
            for i, v in enumerate((sa_bo, ca_bo, ff_b2)):
                sp.dma_start(bias_row[:, i, :], v.rearrange("(a n) -> a n", a=1).broadcast_to([P, D])).then_inc(m_cst, 16)
            with nc.allow_non_contiguous_dma(reason="small vectors by feature"):
                for i, (g_, b_) in enumerate(((ln1_g, ln1_b), (ln2_g, ln2_b), (ln3_g, ln3_b))):
                    sp.dma_start(gb[:, i, 0, :], g_.rearrange("(k p) -> p k", p=P)).then_inc(m_cst, 16)
                    sp.dma_start(gb[:, i, 1, :], b_.rearrange("(k p) -> p k", p=P)).then_inc(m_cst, 16)
                sp.dma_start(b1[:, :], ff_b1.rearrange("(k p) -> p k", p=P)).then_inc(m_cst, 16)
            sp.wait_ge(s_pre, 3)
            sp.dma_start(caq, ca_wq.rearrange("(k p) n -> p k n", p=P)).then_inc(m_caq, 16)
            load_w(0)
            load_wo(0, 0)
            load_wo(1, 0)
            for i in range(16):
                sp.wait_ge(d_pre, 10 + i)
                for l in range(2):
                    if i < 8:
                        src = PT[l][:, i % NPT, :].rearrange("p (n b c) -> p b n c", n=2, b=B)
                        for bb in range(B):
                            move(M_d[l, bb, :, i // 4, 256 * (i % 4):256 * (i % 4) + 256]
                                 .rearrange("p (n c) -> p n c", n=2), src[:, bb], m_scr[i % NPT])
                    else:
                        for bb in range(B):
                            move(VW_d[l, bb, :, i - 8, :], PT[l][:, i % NPT, 256 * bb:256 * bb + 256], m_scr[i % NPT])

            with sp.Fori(0, B) as b:
                sp.wait_ge(s_pre, 25)
                sp.dma_start(X[:, :, :], x[ds(b, 1), :, :].rearrange("a (t p) d -> p (a t) d", p=P)).then_inc(m_x, 16)

                def moves(p, first, last):
                    g, U0 = b * NP + p, b * NU + p * UP
                    if not last:
                        wait_apart(sp, p_w, g + 2)
                        load_w_next(p)
                    if not first:
                        wait_apart(sp, s_pv, NT * U0)
                        load_v(1, p)
                    wait_apart(sp, p_wo[1], g + 1)
                    load_wo_next(1, p)
                    wait_apart(sp, p_wo[0], g + 1)
                    load_wo_next(0, p)
                    if last:
                        return
                    wait_apart(sp, d_qkv, NQ * (g + 1) + 4)
                    wait_apart(sp, s_sc, UT * (U0 + 2))
                    place_qk(0)
                    wait_apart(sp, s_sc, UT * (U0 + 4))
                    place_qk(1)
                    wait_apart(sp, s_pv, NT * (U0 + 2))
                    load_v(0, p + 1)

                def load_w_next(p):
                    nxt = p + 2
                    load_w(nxt if isinstance(nxt, int) and nxt < NP else (nxt % NP if isinstance(nxt, int) else nxt))

                def load_wo_next(h, p):
                    nxt = p + 1
                    load_wo(h, nxt % NP if isinstance(nxt, int) else nxt)

                wait_apart(sp, d_qkv, NQ * (b * NP) + NQ)
                place_qk(0)
                for i in range(NV):
                    wait_apart(sp, d_v, b * NV + i + 1)
                    move(V_d[8 * (i % 2):8 * (i % 2) + 8, :, i // 2, :].rearrange("h p c -> p h c"), vstage[i % 4], m_vst[i % 4])
                for i in range(4):
                    wait_apart(sp, m_vst[i], 16 * (NV // 4) * (b + 1))
                load_v(0, 0)
                load_v(1, 0)
                place_qk(1)
                wait_apart(sp, p_w, b * NP + 1)
                load_w(1)
                moves(0, True, False)
                with sp.Fori(1, NP - 2) as p:
                    moves(p, False, False)
                moves(NP - 2, False, False)
                moves(NP - 1, False, True)
                for i in range(NPT):
                    sp.wait_ge(m_scr[i], 64 * (16 // NPT))
                for h in range(2):
                    wait_apart(sp, m_qk[h], 96 * (b + 1) * NP)
                for l in range(2):
                    move(Mx[l], M_d[l, ds(b, 1)].rearrange("a p k n -> p (a k) n"), m_m)
                wait_apart(sp, s_sc, UT * NU * (b + 1))
                for l in range(2):
                    move(VWx[l], VW_d[l, ds(b, 1)].rearrange("a p n d -> p (a n) d"), m_vw)
                for r in range(2):
                    wait_apart(sp, d_fx, 2 * (2 * b + r + 1))
                    sp.dma_start(out[ds(b, 1), 512 * r:512 * r + 512, :].rearrange("a (t p) d -> p (a t) d", p=P),
                                 X[:, 4 * r:4 * r + 4, :]).then_inc(m_out, 16)
                wait_apart(sp, m_out, 32 * (b + 1))

        @block.gpsimd
        def _(pool):
            def split(raw, hi, lo, count):
                nc.gpsimd.tensor_copy(hi, raw).then_inc(p_wh, 1)
                pool.wait_ge(p_wh, count)
                return nc.gpsimd.tensor_tensor(lo, raw, hi.bitcast(F32), ALU.subtract)

            nc.gpsimd.memset(ident[:, :], 0.0).then_inc(p_id, 1)
            pool.wait_ge(p_id, 1)
            nc.gpsimd.affine_select(out=ident[:, :], in_=ident[:, :], compare_op=ALU.not_equal, fill=1.0,
                                    base=0, pattern=[[-1, P]], channel_multiplier=1).then_inc(p_id, 1)
            nc.gpsimd.memset(kblk, 0.0).then_inc(p_blk, 1)
            nc.gpsimd.memset(vblk, 0.0).then_inc(p_blk, 1)
            pool.wait_ge(m_w, 32)
            split(w_raw[:, :, :, :], w_s[0][:, :, :, :], w_s[1][:, :, :, :], 1).then_inc(p_w, 1)
            def load_chunk(c):
                stage = f_raw[:, c % 2, :]
                if c < 4:
                    dma = pool.dma_start(stage, sa_wv[P * (c // 2):P * (c // 2 + 1), BANK * (c % 2):BANK * (c % 2 + 1)])
                elif c < 12:
                    k, n = (c - 4) // 4, (c - 4) % 4
                    dma = pool.dma_start(stage, ff_w1[P * k:P * (k + 1), BANK * n:BANK * (n + 1)])
                else:
                    dma = pool.dma_start(stage.rearrange("p (f d) -> p f d", d=D),
                                         ff_w2[2 * P * (c - 12):2 * P * (c - 11), :].rearrange("(f p) d -> p f d", p=P))
                dma.then_inc(m_f[c % 2], 16)

            def chunk(l, c):
                if c < 4:
                    return WV[l][:, c // 2, BANK * (c % 2):BANK * (c % 2 + 1)]
                if c < 12:
                    return W1[l][:, (c - 4) // 4, BANK * ((c - 4) % 4):BANK * ((c - 4) % 4 + 1)]
                return W2[l][:, 2 * (c - 12):2 * (c - 11), :].rearrange("p f d -> p (f d)")

            load_chunk(0)
            for c in range(CHUNKS):
                if c + 1 < CHUNKS:
                    if c >= 1:
                        pool.wait_ge(p_f, c)
                    load_chunk(c + 1)
                pool.wait_ge(m_f[c % 2], 16 * (c // 2 + 1))
                done = split(f_raw[:, c % 2, :], chunk(0, c), chunk(1, c), 2 + c)
                done.then_inc(p_f, 1)
            NW0 = 1 + CHUNKS

            with pool.Fori(0, B) as b:
                def add_bias(i):
                    pool.wait_ge(d_z, NT * (3 * b + i + 1))
                    if i == 0:
                        pool.wait_ge(m_cst, 16 * 10)
                    nc.gpsimd.tensor_tensor(X[:, :, :], X[:, :, :],
                                            bias_row[:, i:i + 1, :].to_broadcast([P, NT, D]), ALU.add).then_inc(p_xb, 1)

                def split_wo(h, p, count):
                    g = b * NP + p
                    pool.wait_ge(m_wo[h], 32 * (g + 1))
                    if not (isinstance(p, int) and p == 0):
                        wait_apart(pool, s_op, 2 * UP * g - 4 * (1 - h))
                    else:
                        wait_apart(pool, d_z, NT * (3 * b + 1))
                    split(wo_raw[h][:, :], wo_s[h][0][:, :], wo_s[h][1][:, :], count).then_inc(p_wo[h], 1)

                def split_w(p, count):
                    g = b * NP + p
                    pool.wait_ge(m_w, 32 * (g + 1))
                    wait_apart(pool, s_qkv, NQ * g)
                    split(w_raw[:, :, :, :], w_s[0][:, :, :, :], w_s[1][:, :, :, :], count).then_inc(p_w, 1)

                per_b = 3 * NP + 4
                base = NW0 + b * per_b
                add_bias(0)
                split_wo(0, 0, base + 1)
                split_w(1, base + 2)
                split_wo(1, 0, base + 3)
                with pool.Fori(1, NP - 1) as p:
                    split_wo(0, p, base + 3 * p + 1)
                    split_w(p + 1, base + 3 * p + 2)
                    split_wo(1, p, base + 3 * p + 3)
                split_wo(0, NP - 1, base + 3 * (NP - 1) + 1)
                split_wo(1, NP - 1, base + 3 * (NP - 1) + 2)
                pool.wait_ge(m_w, 32 * ((b + 1) * NP + 1))
                wait_apart(pool, s_qkv, NQ * (b + 1) * NP)
                split(w_raw[:, :, :, :], w_s[0][:, :, :, :], w_s[1][:, :, :, :], base + 3 * NP).then_inc(p_w, 1)
                add_bias(1)
                for t in range(NT):
                    C = b * NT + t
                    pool.wait_ge(d_cr, C + 1)
                    e3 = E[t % 4].rearrange("p (h k) -> p h k", k=T)
                    nc.gpsimd.tensor_tensor(e3, e3, crec[:, t % 2, :].rearrange("p (h a) -> p h a", a=1)
                                            .to_broadcast([P, NH, T]), ALU.mult).then_inc(p_cn, 1)
                add_bias(2)
                wait_apart(pool, s_co, NT * (b + 1))
                for c in range(4):
                    pool.dma_start(f_raw[:, c % 2, :], sa_wv[P * (c // 2):P * (c // 2 + 1), BANK * (c % 2):BANK * (c % 2 + 1)])\
                        .then_inc(m_f[c % 2], 16)
                    wait_apart(pool, m_f[c % 2], 16 * (CHUNKS // 2 + 2 * b + c // 2 + 1))
                    split(f_raw[:, c % 2, :], chunk(0, c), chunk(1, c), base + 3 * NP + 1 + c).then_inc(p_f, 1)

        @block.tensor
        def _(pe):
            mm = nc.tensor.matmul

            pe.wait_ge(p_id, 2)
            pe.wait_ge(m_cnd, 16)
            nc.tensor.transpose(MISC[:, 0:P], cnd[:, 0:P], ident[:, :])
            nc.tensor.transpose(MISC[0:DC - P, P:2 * P], cnd[:, P:DC], ident[:, :]).then_inc(s_pre, 1)
            pe.wait_ge(d_pre, 1)
            pe.wait_ge(m_kv, 64)
            for m, (wa, wb) in enumerate(((wk_a, wk_b), (wv_a, wv_b))):
                for q in range(2):
                    for n in range(4 * q, 4 * q + 4):
                        o = SC[m][:, n * P:(n + 1) * P]
                        mm(o, wa[:, n * P:(n + 1) * P], cndT[:, 0, :], start=True, stop=False)
                        last = mm(o, wb[:, n * P:(n + 1) * P], cndT[0:DC - P, 1, :], start=False, stop=True)
                    last.then_inc(s_pre, 1)
            pe.wait_ge(m_caq, 16)
            for i in range(4):
                bank = (TP[0], TP[1], PV, MISC)[i]
                for n in (2 * i, 2 * i + 1):
                    for k in range(KD):
                        c = (n % 2) * D + k * P
                        last = nc.tensor.transpose(bank[:, c:c + P], caq[:, k, n * P:(n + 1) * P], ident[:, :])
                last.then_inc(s_pre, 1)
            pe.wait_ge(d_pre, 9)
            for i in range(16):
                bank = SC[i // 2 % 2][:, BANK * (i % 2):BANK * (i % 2 + 1)]
                if i >= 4:
                    pe.wait_ge(d_pre, 10 + i - 4)
                if i == 8:
                    pe.wait_ge(m_cao, 16)
                for a in range(2):
                    o = bank[:, 256 * a:256 * a + 256]
                    if i < 8:
                        k, n = i // 4, 2 * (i % 4) + a
                        last = mm(o, wqT[:, n, k * P:(k + 1) * P], kblk[:, n, :, :], start=True, stop=True)
                    else:
                        last = mm(o, vblk[:, i - 8, a, :], X[:, i - 8, :], start=True, stop=True)
                last.then_inc(s_pre, 1)

            def transpose_h(L):
                for n in range(4):
                    r, k = n // 2, n % 2
                    pe.wait_ge(d_z, NT * L + 4 * r + 4)
                    for i in range(4):
                        last = nc.tensor.transpose(SC[r][:, k * BANK + i * P:k * BANK + (i + 1) * P],
                                                   z[:, 4 * r + i, k * P:(k + 1) * P], ident[:, :])
                    last.then_inc(s_tr, 1)

            with pe.Fori(0, B) as b:
                def project(n, bank):
                    kind, half = PROJ[n]
                    m = "qk".index(kind)
                    for c, (l, r) in enumerate(TERMS):
                        for k in range(KD):
                            last = mm(bank[:, :], w_s[l][:, m, k, :], hT[r][:, k, half * BANK:(half + 1) * BANK],
                                      start=(c == 0 and k == 0), stop=(c == 2 and k == KD - 1))
                    last.then_inc(s_qkv, 1)

                def scores(tau):
                    h, qt = tau // 8 % 2, tau % 8
                    for half in range(2):
                        for l in range(2):
                            last = mm(SC[tau % 2][:, half * BANK:(half + 1) * BANK], QKS[:, 3 * h, qt * P:(qt + 1) * P],
                                      QKS[:, 3 * h + 1 + l, half * BANK:(half + 1) * BANK], start=(l == 0), stop=(l == 1))
                    last.then_inc(s_sc, 1)

                def attend(U, s, j):
                    h = s // 2
                    pe.wait_ge(d_pl, NT * U + j + 1)
                    for l in range(2):
                        last = mm(PV[:, :], VS[h][:, j, :], PT[l][:, j % NPT, :], start=(j == 0 and l == 0),
                                  stop=(j == NT - 1 and l == 1))
                    last.then_inc(s_pv, 1)

                def project_out(U, h, k):
                    for i in (2 * k, 2 * k + 1):
                        for c, (l, r) in enumerate(TERMS):
                            last = mm(MISC[:, D * (i % 2):D * (i % 2) + D], OT[l][:, i * P:(i + 1) * P],
                                      wo_s[h][r][:, :], start=(c == 0), stop=(c == 2))
                    last.then_inc(s_op, 1)

                transpose_h(3 * b)
                pe.wait_ge(d_hl, 4 * (3 * b) + 4)
                pe.wait_ge(p_w, b * NP + 1)
                for n in range(NQ):
                    project(n, (MISC, PV, TP[0], TP[1])[n])
                pe.wait_ge(p_f, 4 + b * CHUNKS)
                for i in range(NV):
                    bank = (SC[0][:, 0:BANK], SC[0][:, BANK:2 * BANK], SC[1][:, 0:BANK], SC[1][:, BANK:2 * BANK])[i % 4]
                    if i >= 4:
                        pe.wait_ge(d_v, b * NV + i - 3)
                    for c, (l, r) in enumerate(TERMS):
                        for k in range(KD):
                            last = mm(bank, hT[l][:, k, i // 2 * P:(i // 2 + 1) * P], WV[r][:, k, i % 2 * BANK:(i % 2 + 1) * BANK],
                                      start=(c == 0 and k == 0), stop=(c == 2 and k == KD - 1))
                    last.then_inc(s_v, 1)
                pe.wait_ge(d_v, NV * (b + 1))
                pe.wait_ge(m_qk[0], 96 * (b * NP + 1))
                for tau in range(5):
                    if tau >= 2:
                        pe.wait_ge(a_exp, UT * NU * b + tau - 1)
                    scores(tau)

                def pair(p, first, last):
                    g, U0 = b * NP + p, b * NU + p * UP
                    for s in range(UP):
                        U = U0 + s
                        for j in range(NT):
                            if j == 0:
                                pe.wait_ge(a_exp, UT * U + UT)
                            if not (first and s == 0 and j < 2):
                                pe.wait_ge(d_pl, NT * U + j - 1)
                            for i in range(UT):
                                tr = nc.tensor.transpose(TP[j % 2][:, i * P:(i + 1) * P],
                                                         PR[:, s % 2, i, j * P:(j + 1) * P], ident[:, :])
                            tr.then_inc(s_pt, 1)
                            if j < 3 and not (first and s == 0):
                                attend(U - 1, (s - 1) % UP, j + 5)
                            if j == 4:
                                if s == 0:
                                    pe.wait_ge(m_v[0], 16 * (g + 1))
                                if s == 2:
                                    pe.wait_ge(m_v[1], 16 * (g + 1))
                                if not (first and s == 0):
                                    pe.wait_ge(d_ol, U)
                                attend(U, s, 0)
                            if j >= 4:
                                attend(U, s, j - 3)
                            tau = UT * s + 5 + j // 2
                            if j % 2 == 1 and not (last and tau >= 16):
                                pe.wait_ge(a_exp, UT * U0 + tau - 1)
                                if tau == 8:
                                    pe.wait_ge(m_qk[1], 96 * (g + 1))
                                if tau == 16:
                                    pe.wait_ge(m_qk[0], 96 * (g + 2))
                                scores(tau)
                            if j in (1, 3) and s < 2 and not last:
                                n = 2 * s + j // 2
                                if n == 0:
                                    pe.wait_ge(p_w, g + 2)
                                if j == 3 or (first and s < 2):
                                    pe.wait_ge(d_qkv, NQ * (g + 1) + n)
                                else:
                                    pe.wait_ge(d_x, 2 * U - 2)
                                project(n, MISC)
                            if j in (5, 7) and not (first and s == 0):
                                if j == 5:
                                    pe.wait_ge(d_ol, U)
                                    if s % 2 == 1:
                                        pe.wait_ge(p_wo[s // 2], g + 1)
                                    if s < 2 and not last:
                                        pe.wait_ge(d_qkv, NQ * (g + 1) + 2 * s + 2)
                                    elif not (first and s == 1):
                                        pe.wait_ge(d_x, 2 * U - 2)
                                else:
                                    pe.wait_ge(d_x, 2 * U - 1)
                                project_out(U - 1, (s - 1) % UP // 2, (j - 5) // 2)

                pair(0, True, False)
                with pe.Fori(1, NP - 1) as p:
                    pair(p, False, False)
                pair(NP - 1, False, True)
                UE = (b + 1) * NU
                for j in range(5, 8):
                    attend(UE - 1, 3, j)
                pe.wait_ge(d_ol, UE)
                for k in range(2):
                    pe.wait_ge(d_x, 2 * UE - 2 + k)
                    project_out(UE - 1, 1, k)

                transpose_h(3 * b + 1)
                pe.wait_ge(d_hl, 4 * (3 * b + 1) + 4)
                pe.wait_ge(m_m, 32 * (b + 1))
                for t in range(NT + 3):
                    C = b * NT + t
                    if t < NT:
                        if t >= 2:
                            pe.wait_ge(d_cs, C - 1)
                        for half in range(2):
                            for c, (l, r) in enumerate(TERMS):
                                for k in range(KD):
                                    last = mm(SC[t % 2][:, half * BANK:(half + 1) * BANK], hT[l][:, k, t * P:(t + 1) * P],
                                              Mx[r][:, k, half * BANK:(half + 1) * BANK],
                                              start=(c == 0 and k == 0), stop=(c == 2 and k == KD - 1))
                        last.then_inc(s_cs, 1)
                    if 2 <= t < NT + 2:
                        pe.wait_ge(p_cn, C - 1)
                        for k in range(2):
                            if t > 2:
                                pe.wait_ge(d_cl, 2 * (C - 2) + k - 1)
                            for i in range(4):
                                last = nc.tensor.transpose(TP[k][:, i * P:(i + 1) * P],
                                                           E[(t - 2) % 4][:, (4 * k + i) * P:(4 * k + i + 1) * P], ident[:, :])
                            last.then_inc(s_ct, 1)
                    if t >= 3:
                        if t == 3:
                            pe.wait_ge(m_vw, 32 * (b + 1))
                        if t >= 5:
                            pe.wait_ge(d_cx, C - 4)
                        pe.wait_ge(d_cl, 2 * (C - 3) + 2)
                        for n in range(NP):
                            for c, (l, r) in enumerate(TERMS):
                                last = mm((PV, MISC)[(t - 3) % 2][:, 0:D],
                                          PT[l][:, (2 * (t - 3) + n // 4) % NPT, (n % 4) * P:(n % 4 + 1) * P], VWx[r][:, n, :],
                                          start=(n == 0 and c == 0), stop=(n == NP - 1 and c == 2))
                        last.then_inc(s_co, 1)

                transpose_h(3 * b + 2)
                pe.wait_ge(d_hl, 4 * (3 * b + 2) + 4)
                pe.wait_ge(p_f, CHUNKS)

                def ff_down(F, r, f):
                    pe.wait_ge(d_ul, F + 1)
                    for i in range(4):
                        bank = ((TP[0], TP[1]), (PV, MISC))[r][i // 2]
                        for c, (l, m) in enumerate(TERMS):
                            last = mm(bank[:, D * (i % 2):D * (i % 2) + D], PT[l][:, f % NPT, i * P:(i + 1) * P],
                                      W2[m][:, f, :], start=(f == 0 and c == 0 and i % 2 == 0),
                                      stop=(f == NF - 1 and c == 2), skip_group_check=True)
                    last.then_inc(s_w2, 1)

                for r in range(2):
                    for f in range(NF + 2):
                        F = b * 2 * NF + r * NF + f
                        if f < NF:
                            if r or f >= 2:
                                pe.wait_ge(d_u, F - 1)
                            for part, col in enumerate((FF + f * P, f * P)):
                                for c, (l, m) in enumerate(TERMS):
                                    for k in range(KD):
                                        last = mm(SC[f % 2][:, part * BANK:(part + 1) * BANK], W1[l][:, k, col:col + P],
                                                  hT[m][:, k, r * BANK:(r + 1) * BANK],
                                                  start=(c == 0 and k == 0), stop=(c == 2 and k == KD - 1))
                            last.then_inc(s_ff, 1)
                        if f >= 2:
                            ff_down(F - 2, r, f - 2)

        @block.scalar
        def _(act):
            for i in range(16):
                bank = SC[i // 2 % 2][:, BANK * (i % 2):BANK * (i % 2 + 1)]
                act.wait_ge(s_pre, 10 + i)
                if i >= NPT:
                    act.wait_ge(m_scr[i % NPT], 64 * (i // NPT))
                nc.scalar.copy(PT[0][:, i % NPT, :], bank).then_inc(a_pre, 1)

            for i in range(NPT):
                act.wait_ge(m_scr[i], 64 * (16 // NPT))
            with act.Fori(0, B) as b:
                def norm(L):
                    act.wait_ge(d_mv, NT * (L + 1))
                    nc.scalar.activation(sd[:, :], mv[:, :, 1], ACT.Sqrt, bias=EPS).then_inc(a_sd, 1)
                    for n in range(4):
                        r, k = n // 2, n % 2
                        act.wait_ge(d_h, 4 * L + n + 1)
                        nc.scalar.copy(hT[0][:, k, r * BANK:(r + 1) * BANK], h32[:, k, r * BANK:(r + 1) * BANK]).then_inc(a_hh, 1)

                def split_qkv(g, n, bank):
                    kind, half = PROJ[n]
                    act.wait_ge(s_qkv, NQ * g + n + 1)
                    nc.scalar.mul(QKT[:, 2 * "qk".index(kind), half * BANK:(half + 1) * BANK], bank[:, :],
                                  SCALE if kind == "q" else 1.0).then_inc(a_qkv, 1)

                def exp(U0, tau):
                    u = tau // UT
                    act.wait_ge(d_max, UT * U0 + tau + 1)
                    nc.scalar.activation(PR[:, u % 2, tau % UT, :], SC[tau % 2][:, :], ACT.Exp,
                                         bias=nmax[:, tau % 4:tau % 4 + 1],
                                         accum_out=den[:, u % 2, tau % UT:tau % UT + 1]).then_inc(a_exp, 1)

                def split_out(U, first):
                    act.wait_ge(s_pv, NT * U + NT)
                    if not first:
                        act.wait_ge(s_op, 2 * U)
                    nc.scalar.copy(OT[0][:, :], PV[:, :]).then_inc(a_oh, 1)

                norm(3 * b)
                for n in range(NQ):
                    split_qkv(b * NP, n, (MISC, PV, TP[0], TP[1])[n])
                for i in range(NV):
                    act.wait_ge(s_v, b * NV + i + 1)
                    if i >= 4:
                        act.wait_ge(m_vst[i % 4], 16 * (b * (NV // 4) + i // 4))
                    nc.scalar.copy(vstage[i % 4][:, :, 0:DH],
                                   SC[i % 4 // 2][:, BANK * (i % 2):BANK * (i % 2 + 1)].rearrange("p (h d) -> p h d", d=DH))\
                        .then_inc(a_v, 1)
                for tau in range(5):
                    exp(b * NU, tau)

                def pair(p, first, last):
                    g, U0 = b * NP + p, b * NU + p * UP
                    for s in range(UP):
                        U = U0 + s
                        for j in range(NT):
                            act.wait_ge(s_pt, NT * U + j + 1)
                            if not (first and s == 0 and j < NPT):
                                act.wait_ge(s_pv, NT * U + j - NPT + 1)
                            nc.scalar.copy(PT[0][:, j % NPT, :], TP[j % 2][:, :]).then_inc(a_ph, 1)
                            if j == 3 and not (first and s == 0):
                                split_out(U - 1, first and s == 1)
                            if j in (2, 4) and s < 2 and not last:
                                n = 2 * s + j // 2 - 1
                                if n == 0:
                                    act.wait_ge(m_qk[1], 96 * (g + 1))
                                    act.wait_ge(m_qk[0], 96 * (g + 1))
                                split_qkv(g + 1, n, MISC)
                            tau = UT * s + 4 + j // 2
                            if j % 2 == 0 and not (first and s == 0 and j == 0) and not (last and tau >= 16):
                                if j == 0:
                                    act.wait_ge(d_rd, U)
                                exp(U0, tau)

                pair(0, True, False)
                with act.Fori(1, NP - 1) as p:
                    pair(p, False, False)
                pair(NP - 1, False, True)
                split_out((b + 1) * NU - 1, False)

                norm(3 * b + 1)
                for t in range(NT + 2):
                    C = b * NT + t
                    if t < NT:
                        act.wait_ge(d_cs, C + 1)
                        nc.scalar.activation(E[t % 4], E[t % 4], ACT.Exp).then_inc(a_ce, 1)
                    if t >= 2:
                        for k in range(2):
                            act.wait_ge(s_ct, 2 * (C - 2) + k + 1)
                            if t >= 4:
                                act.wait_ge(s_co, C - 3)
                            nc.scalar.copy(PT[0][:, (2 * (t - 2) + k) % NPT, :], TP[k][:, :]).then_inc(a_ch, 1)

                norm(3 * b + 2)
                for r in range(2):
                    for f in range(NF + 1):
                        F = b * 2 * NF + r * NF + f
                        if f < NF:
                            act.wait_ge(s_ff, F + 1)
                            if r or f >= 2:
                                act.wait_ge(d_u, F - 1)
                            nc.scalar.activation(G[f % 2], SC[f % 2][:, 0:BANK], ACT.Gelu,
                                                 bias=b1[:, NF + f:NF + f + 1]).then_inc(a_g, 1)
                        if f >= 1:
                            act.wait_ge(d_u, F)
                            if r or f - 1 >= NPT:
                                act.wait_ge(s_w2, F - NPT)
                            nc.scalar.copy(PT[0][:, (f - 1) % NPT, :], U32[(f - 1) % 2]).then_inc(a_uh, 1)

        @block.vector
        def _(dve):
            V = nc.vector
            sub = ALU.subtract

            dve.wait_ge(s_pre, 1)
            V.tensor_copy(cndT[:, 0, :], MISC[:, 0:P])
            V.tensor_copy(cndT[0:DC - P, 1, :], MISC[0:DC - P, P:2 * P]).then_inc(d_pre, 1)
            dve.wait_ge(p_blk, 2)
            for m, blk in enumerate((kblk, vblk)):
                for q in range(2):
                    dve.wait_ge(s_pre, 2 + 2 * m + q)
                    for h in range(2):
                        rows = slice(64 * h, 64 * h + 64)
                        src = SC[m][rows, q * BANK:(q + 1) * BANK].rearrange("p (n b c) -> p n b c", n=4, b=B)
                        last = V.tensor_scalar(blk[rows, 4 * q:4 * q + 4, :, 64 * h:64 * h + 64], src,
                                               (SCALE, 1.0)[m], None, ALU.mult)
                    last.then_inc(d_pre, 1)
            for i in range(4):
                dve.wait_ge(s_pre, 6 + i)
                V.tensor_copy(wqT[:, 2 * i:2 * i + 2, :].rearrange("p n c -> p (n c)"),
                              (TP[0], TP[1], PV, MISC)[i][:, :]).then_inc(d_pre, 1)
            for i in range(16):
                bank = SC[i // 2 % 2][:, BANK * (i % 2):BANK * (i % 2 + 1)]
                dve.wait_ge(a_pre, i + 1)
                V.tensor_tensor(PT[1][:, i % NPT, :], bank, PT[0][:, i % NPT, :].bitcast(F32), sub).then_inc(d_pre, 1)

            with dve.Fori(0, B) as b:
                def norm(L, i):
                    for t in range(NT):
                        V.bn_stats(st[:, t, :], X[:, t, :]).then_inc(d_st, 1)
                    wait_apart(dve, d_st, NT * (L + 1))
                    for t in range(NT):
                        V.bn_aggr(mv[:, t, :], st[:, t, :]).then_inc(d_mv, 1)
                    dve.wait_ge(a_sd, L + 1)
                    V.reciprocal(rs[:, :], sd[:, :]).then_inc(d_rs, 1)
                    dve.wait_ge(d_rs, L + 1)
                    for t in range(NT):
                        V.tensor_scalar(z[:, t, :], X[:, t, :], mv[:, t, 0:1], rs[:, t:t + 1], sub, ALU.mult).then_inc(d_z, 1)
                    for n in range(5):
                        r, k = n // 2, n % 2
                        if n < 4:
                            dve.wait_ge(s_tr, 4 * L + n + 1)
                            V.tensor_scalar(h32[:, k, r * BANK:(r + 1) * BANK], SC[r][:, k * BANK:(k + 1) * BANK],
                                            gb[:, i, 0, k:k + 1], gb[:, i, 1, k:k + 1], ALU.mult, ALU.add).then_inc(d_h, 1)
                        if n >= 1:
                            r, k = (n - 1) // 2, (n - 1) % 2
                            dve.wait_ge(a_hh, 4 * L + n)
                            V.tensor_tensor(hT[1][:, k, r * BANK:(r + 1) * BANK], h32[:, k, r * BANK:(r + 1) * BANK],
                                            hT[0][:, k, r * BANK:(r + 1) * BANK].bitcast(F32), sub).then_inc(d_hl, 1)

                def split_qkv(g, n, bank):
                    kind, half = PROJ[n]
                    dve.wait_ge(a_qkv, NQ * g + n + 1)
                    m, cols = 2 * "qk".index(kind), slice(half * BANK, (half + 1) * BANK)
                    V.scalar_tensor_tensor(QKT[:, m + 1, cols], bank[:, :], SCALE if kind == "q" else 1.0,
                                           QKT[:, m, cols].bitcast(F32), ALU.mult, sub).then_inc(d_qkv, 1)

                def rowmax(U0, tau, fresh):
                    dve.wait_ge(s_sc, UT * U0 + tau + 1)
                    if not fresh:
                        dve.wait_ge(a_exp, UT * U0 + tau - 3)
                    V.tensor_reduce(nmax[:, tau % 4:tau % 4 + 1], SC[tau % 2][:, :], AX, ALU.max, negate=True).then_inc(d_max, 1)

                def split_out(U):
                    dve.wait_ge(a_oh, U + 1)
                    V.tensor_tensor(OT[1][:, :], PV[:, :], OT[0][:, :].bitcast(F32), sub).then_inc(d_ol, 1)

                def add_out(U, s, k):
                    dve.wait_ge(s_op, 2 * U + k + 1)
                    for i in (2 * k, 2 * k + 1):
                        t = UT * (s % 2) + i
                        last = V.scalar_tensor_tensor(X[:, t, :], MISC[:, D * (i % 2):D * (i % 2) + D],
                                                      rden[:, s % 2, i:i + 1], X[:, t, :], ALU.mult, ALU.add)
                    last.then_inc(d_x, 1)

                dve.wait_ge(m_x, 16 * (b + 1))
                dve.wait_ge(m_cst, 160)
                norm(3 * b, 0)
                for n in range(NQ):
                    split_qkv(b * NP, n, (MISC, PV, TP[0], TP[1])[n])
                for i in range(NV):
                    dve.wait_ge(a_v, b * NV + i + 1)
                    V.tensor_tensor(vstage[i % 4][:, :, DH:P],
                                    SC[i % 4 // 2][:, BANK * (i % 2):BANK * (i % 2 + 1)].rearrange("p (h d) -> p h d", d=DH),
                                    vstage[i % 4][:, :, 0:DH].bitcast(F32), sub).then_inc(d_v, 1)
                for tau in range(5):
                    rowmax(b * NU, tau, tau < 4)
                dve.wait_ge(p_xb, 3 * b + 1)

                def pair(p, first, last):
                    g, U0 = b * NP + p, b * NU + p * UP
                    for s in range(UP):
                        U = U0 + s
                        for j in range(NT):
                            dve.wait_ge(a_ph, NT * U + j + 1)
                            V.tensor_tensor(PT[1][:, j % NPT, :], TP[j % 2][:, :], PT[0][:, j % NPT, :].bitcast(F32),
                                            sub).then_inc(d_pl, 1)
                            tau = UT * s + 5 + j // 2
                            if j == 3 and not (first and s == 0):
                                split_out(U - 1)
                            if j % 2 == 1 and not (last and tau >= 16):
                                rowmax(U0, tau, False)
                            if j == 1:
                                dve.wait_ge(a_exp, UT * U + UT)
                                if not (first and s < 2):
                                    dve.wait_ge(d_x, 2 * U - 2)
                                V.reciprocal(rden[:, s % 2, :], den[:, s % 2, :]).then_inc(d_rd, 1)
                            if j == 0 and not (first and s < 2):
                                add_out(U - 2, (s - 2) % UP, 1)
                            if j in (2, 4) and s < 2 and not last:
                                split_qkv(g + 1, 2 * s + j // 2 - 1, MISC)
                            if j == 6 and not (first and s == 0):
                                add_out(U - 1, (s - 1) % UP, 0)

                pair(0, True, False)
                with dve.Fori(1, NP - 1) as p:
                    pair(p, False, False)
                pair(NP - 1, False, True)
                add_out((b + 1) * NU - 2, 2, 1)
                split_out((b + 1) * NU - 1)
                for k in range(2):
                    add_out((b + 1) * NU - 1, 3, k)
                dve.wait_ge(d_x, 2 * NU * (b + 1))

                norm(3 * b + 1, 1)
                dve.wait_ge(p_xb, 3 * b + 2)
                for t in range(NT + 3):
                    C = b * NT + t
                    if t < NT:
                        ps3 = SC[t % 2][:, :].rearrange("p (h k) -> p h k", k=T)
                        bc = lambda v: v[:, t % 2, :].rearrange("p (h a) -> p h a", a=1).to_broadcast([P, NH, T])
                        dve.wait_ge(s_cs, C + 1)
                        V.tensor_reduce(cmax[:, t % 2, :], ps3, AX, ALU.max).then_inc(d_cm, 1)
                        dve.wait_ge(d_cm, C + 1)
                        if t >= 4:
                            dve.wait_ge(s_ct, 2 * (C - 3))
                        V.tensor_tensor(E[t % 4].rearrange("p (h k) -> p h k", k=T), ps3, bc(cmax), sub).then_inc(d_cs, 1)
                    if 1 <= t < NT + 1:
                        dve.wait_ge(a_ce, C)
                        V.tensor_reduce(csum[:, (t - 1) % 2, :], E[(t - 1) % 4].rearrange("p (h k) -> p h k", k=T),
                                        AX, ALU.add).then_inc(d_csum, 1)
                        dve.wait_ge(d_csum, C)
                        if t >= 3:
                            dve.wait_ge(p_cn, C - 2)
                        V.reciprocal(crec[:, (t - 1) % 2, :], csum[:, (t - 1) % 2, :]).then_inc(d_cr, 1)
                    if 2 <= t < NT + 2:
                        for k in range(2):
                            dve.wait_ge(a_ch, 2 * (C - 2) + k + 1)
                            slot = (2 * (t - 2) + k) % NPT
                            V.tensor_tensor(PT[1][:, slot, :], TP[k][:, :], PT[0][:, slot, :].bitcast(F32), sub).then_inc(d_cl, 1)
                    if t >= 3:
                        dve.wait_ge(s_co, C - 2)
                        V.tensor_tensor(X[:, t - 3, :], (PV, MISC)[(t - 3) % 2][:, 0:D], X[:, t - 3, :], ALU.add).then_inc(d_cx, 1)
                dve.wait_ge(d_cx, NT * (b + 1))

                norm(3 * b + 2, 2)
                dve.wait_ge(p_xb, 3 * b + 3)
                for r in range(2):
                    for f in range(NF + 1):
                        F = b * 2 * NF + r * NF + f
                        if f < NF:
                            dve.wait_ge(a_g, F + 1)
                            if r or f >= 2:
                                dve.wait_ge(d_ul, F - 1)
                            V.scalar_tensor_tensor(U32[f % 2], SC[f % 2][:, BANK:2 * BANK], b1[:, f:f + 1], G[f % 2],
                                                   ALU.add, ALU.mult).then_inc(d_u, 1)
                        if f >= 1:
                            dve.wait_ge(a_uh, F)
                            V.tensor_tensor(PT[1][:, (f - 1) % NPT, :], U32[(f - 1) % 2],
                                            PT[0][:, (f - 1) % NPT, :].bitcast(F32), sub).then_inc(d_ul, 1)
                    dve.wait_ge(s_w2, NF * (2 * b + r + 1))
                    for i in range(2):
                        xs = X[:, 4 * r + 2 * i:4 * r + 2 * i + 2, :].rearrange("p t d -> p (t d)")
                        V.tensor_tensor(xs, ((TP[0], TP[1]), (PV, MISC))[r][i][:, :], xs, ALU.add).then_inc(d_fx, 1)


_INS = ['x', 'ctx_768'] + ['L0_xattn_' + n for n in (
    'ln1_g', 'ln1_b', 'ln2_g', 'ln2_b', 'ln3_g', 'ln3_b', 'sa_wq', 'sa_wk', 'sa_wv', 'sa_wo', 'sa_bo',
    'ca_wq', 'ca_wk', 'ca_wv', 'ca_wo', 'ca_bo', 'ff_w1', 'ff_b1', 'ff_w2', 'ff_b2')]
_OUTS = [((2, 1024, 256), 'float32')]


def kernel(**inputs):
    import numpy as _np
    import concourse.bacc as _bacc
    from concourse import mybir as _mybir
    from concourse.bass_utils import run_bass_kernel_spmd as _run

    nc = _bacc.Bacc("TRN2", target_bir_lowering=False, num_devices=1)
    arrays, args = {}, []
    for name in _INS:
        a = _np.ascontiguousarray(inputs[name])
        arrays[f"in_{name}_dram"] = a
        args.append(nc.dram_tensor(f"in_{name}_dram", a.shape, _mybir.dt.from_np(a.dtype), kind="ExternalInput").ap())
    for i, (shape, dtype) in enumerate(_OUTS):
        dt = _mybir.dt.from_np(_np.dtype(dtype))
        args.append(nc.dram_tensor(f"out_{i}_dram", shape, dt, kind="ExternalOutput").ap())
    build_block(nc, *args)
    r = _run(nc, [arrays], core_ids=[0])
    got = tuple(r.results[0][f"out_{i}_dram"] for i in range(len(_OUTS)))
    return got[0]
```

```python
from contextlib import ExitStack

import concourse.bass as bass
from concourse import mybir

F32 = mybir.dt.float32
F32R = mybir.dt.float32r
ALU = mybir.AluOpType
ACT = mybir.ActivationFunctionType
AX = mybir.AxisListType.X
ds = bass.ds

P = 128
BANK = 512
EPS = 1e-5


def build_block(nc, x, cond, ln1_g, ln1_b, ln2_g, ln2_b, ln3_g, ln3_b, sa_wq, sa_wk, sa_wv, sa_wo, sa_bo,
                ca_wq, ca_wk, ca_wv, ca_wo, ca_bo, ff_w1, ff_b1, ff_w2, ff_b2, out):
    B, S, D = x.shape
    T, DC = cond.shape[1:]
    DA = sa_wq.shape[1]
    FF = ff_w2.shape[0]
    DH = 64
    NH = DA // DH
    NP = NH // 2
    NT = S // P
    KD = D // P
    NF = FF // P
    UP = 4
    NU = NP * UP
    UT = 4
    NPT = 4
    SCALE = float(DH) ** -0.5
    assert (B, S, D, T, DC, DA, FF) == (2, 1024, 256, 64, 192, 1024, 1024)

    with ExitStack() as ctx:
        def sb(name, shape, dt=F32):
            return ctx.enter_context(nc.sbuf_tensor(name, shape, dt))

        def sem(name):
            return ctx.enter_context(nc.semaphore(name))

        X = sb("X", [P, NT, D])
        hT = [sb("hT_hi", [P, KD, S], F32R), sb("hT_lo", [P, KD, S], F32R)]
        PR = sb("PR", [P, 2, UT, S])
        PT = [sb("PT_hi", [P, NPT, BANK], F32R), sb("PT_lo", [P, NPT, BANK], F32R)]
        QKT = sb("QKT", [P, 4, S], F32R)
        QKS = sb("QKS", [P, 6, S], F32R)
        VS = [sb(f"VS{h}", [P, NT, P], F32R) for h in range(2)]
        VX = sb("VX", [P, NT, P], F32R)
        WV_hi = sb("WV_hi", [P, KD, DA], F32R)
        OT = [sb("OT_hi", [P, BANK], F32R), sb("OT_lo", [P, BANK], F32R)]
        w_raw = sb("w_raw", [P, 2, KD, P])
        w_s = [sb("w_hi", [P, 2, KD, P], F32R), sb("w_lo", [P, 2, KD, P], F32R)]
        wo_raw = [sb(f"wo_raw{h}", [P, D]) for h in range(2)]
        wo_s = [[sb(f"wo_hi{h}", [P, D], F32R), sb(f"wo_lo{h}", [P, D], F32R)] for h in range(2)]
        W1 = [sb("W1_hi", [P, KD, 2 * FF], F32R), sb("W1_lo", [P, KD, 2 * FF], F32R)]
        W2 = [sb("W2_hi", [P, NF, D], F32R), sb("W2_lo", [P, NF, D], F32R)]
        ident = sb("ident", [P, P])
        bias_row = sb("bias_row", [P, 3, D])
        gb = sb("gb", [P, 3, 2, KD])
        b1 = sb("b1", [P, 2 * NF])
        f_raw = sb("f_raw", [P, 2, BANK])
        cnd = sb("cnd", [P, DC])
        cndT = sb("cndT", [P, 2, P])
        st = sb("st", [P, NT, 6])
        mv = sb("mv", [P, NT, 2])
        sd = sb("sd", [P, NT])
        rs = sb("rs", [P, NT])
        nmax = sb("nmax", [P, 4])
        den = sb("den", [P, 2, UT])
        rden = sb("rden", [P, 2, UT])
        cmax = sb("cmax", [P, 2, NH])
        csum = sb("csum", [P, 2, NH])
        crec = sb("crec", [P, 2, NH])

        M_d = nc.dram_tensor("scratch_m", [2, B, P, KD, DA], F32, kind="Internal").ap()
        VW_d = nc.dram_tensor("scratch_vw", [2, B, P, NP, D], F32, kind="Internal").ap()

        V_d = nc.dram_tensor("scratch_v", [NH, P, NT, P], F32, kind="Internal").ap()

        SC = [ctx.enter_context(nc.psum_tensor(f"SC{i}", [P, 2 * BANK], F32)) for i in range(2)]
        TP = [ctx.enter_context(nc.psum_tensor(f"TP{i}", [P, BANK], F32)) for i in range(2)]
        PV = ctx.enter_context(nc.psum_tensor("PV", [P, BANK], F32))
        MISC = ctx.enter_context(nc.psum_tensor("MISC", [P, BANK], F32))

        prf = PR[:, :, :, :].rearrange("p a b n -> p (a b) n")
        z = PR[:, 0, 0:2, :].rearrange("p a n -> p (a n)").rearrange("p (t d) -> p t d", d=D)
        h32 = PR[:, 0, 2:4, :]
        wk_a, wk_b, wv_a, wv_b = prf[:, 0, :], prf[0:DC - P, 1, :], prf[:, 2, :], prf[0:DC - P, 3, :]
        kblk = prf[:, 4:6, :].rearrange("p a n -> p (a n)").rearrange("p (n b c) -> p n b c", n=NP, b=B)
        vblk = prf[:, 6:8, :].rearrange("p a n -> p (a n)").rearrange("p (n b c) -> p n b c", n=NP, b=B)
        caq = prf[:, 0:2, :]
        wqT = prf[:, 2:4, :].rearrange("p a n -> p (a n)").rearrange("p (n c) -> p n c", c=D)
        E = [PR[:, 1, i, :] for i in range(4)]
        G = [PR[:, 1, 2, i * BANK:(i + 1) * BANK] for i in range(2)]
        U32 = [PR[:, 1, 3, i * BANK:(i + 1) * BANK] for i in range(2)]
        XN = PR[:, 1, 0:2, :].rearrange("p a n -> p (a n)").rearrange("p (t d) -> p t d", d=D)
        HB = [[SC[0][:, 0:BANK], SC[0][:, BANK:2 * BANK]], [PV[:, :], MISC[:, :]]]
        WV = [WV_hi, QKS[:, 4:6, :]]
        vstage = [VS[0][:, :, :], VS[1][:, :, :], VX[:, :, :], QKS[:, 3, :].rearrange("p (k c) -> p k c", c=P)]
        VB = (MISC, PV, TP[0], TP[1])
        NV = 2 * NT
        Mx = [QKT[:, 0:2, :], QKT[:, 2:4, :]]
        vwf = QKS[:, 0:4, :].rearrange("p a n -> p (a n)").rearrange("p (l n d) -> p l n d", l=2, d=D)
        VWx = [vwf[:, 0], vwf[:, 1]]

        m_x = sem("m_x"); x_free = sem("x_free"); m_out = sem("m_out"); m_cst = sem("m_cst"); m_cnd = sem("m_cnd")
        m_kv = sem("m_kv"); m_caq = sem("m_caq"); m_cao = sem("m_cao"); m_scr = [sem(f"m_scr{i}") for i in range(4)]
        m_w = sem("m_w"); m_wo = [sem("m_wo0"), sem("m_wo1")]; m_f = [sem("m_f0"), sem("m_f1")]
        m_qk = [sem("m_qk0"), sem("m_qk1")]; m_q1 = [sem("m_q10"), sem("m_q11")]; m_v = [sem("m_v0"), sem("m_v1")]
        m_m = sem("m_m"); m_vw = sem("m_vw")
        waited = sem("waited")
        p_id = sem("p_id"); p_blk = sem("p_blk")
        p_w = sem("p_w"); p_wo = [sem("p_wo0"), sem("p_wo1")]; p_f = sem("p_f"); p_wh = sem("p_wh")
        p_xb = sem("p_xb"); p_cn = sem("p_cn")
        s_pre = sem("s_pre"); d_pre = sem("d_pre"); a_pre = sem("a_pre")
        d_st = sem("d_st"); d_mv = sem("d_mv"); a_sd = sem("a_sd"); d_rs = sem("d_rs"); d_z = sem("d_z")
        s_tr = sem("s_tr"); d_h = sem("d_h"); a_hh = sem("a_hh"); d_hl = sem("d_hl")
        s_sc = sem("s_sc"); d_max = sem("d_max"); a_exp = sem("a_exp"); d_rd = sem("d_rd")
        s_pt = sem("s_pt"); a_ph = sem("a_ph"); d_pl = sem("d_pl"); s_pv = sem("s_pv")
        a_oh = sem("a_oh"); d_ol = sem("d_ol"); s_op = sem("s_op"); d_x = sem("d_x")
        s_qkv = sem("s_qkv"); a_qkv = sem("a_qkv"); d_qkv = sem("d_qkv")
        p_wv = sem("p_wv"); s_v = sem("s_v"); a_v = sem("a_v"); d_v = sem("d_v"); m_vst = [sem(f"m_vst{i}") for i in range(4)]
        s_cs = sem("s_cs"); d_cm = sem("d_cm"); d_cs = sem("d_cs"); a_ce = sem("a_ce")
        d_csum = sem("d_csum"); d_cr = sem("d_cr"); s_ct = sem("s_ct"); a_ch = sem("a_ch"); d_cl = sem("d_cl")
        s_co = sem("s_co"); d_cx = sem("d_cx")
        s_ff = sem("s_ff"); a_g = sem("a_g"); d_u = sem("d_u"); a_uh = sem("a_uh"); d_ul = sem("d_ul")
        s_w2 = sem("s_w2"); d_fx = sem("d_fx")

        TERMS = [(0, 0), (0, 1), (1, 0)]

        PROJ = [("q", 0), ("k", 0), ("k", 1), ("q", 1)]
        NQ = len(PROJ)
        CHUNKS = 16

        def wait_apart(eng, signal, value):
            eng.wait_ge(signal, value)
            eng.sem_inc(waited, 1)

        block = ctx.enter_context(nc.Block())

        @block.sync
        def _(sp):
            def move(to, of, signal):
                sp.dma_start(to.bitcast(F32), of.bitcast(F32)).then_inc(signal, 16)

            def load_w(p):
                for m, w in enumerate((sa_wq, sa_wk)):
                    sp.dma_start(w_raw[:, m, :, :], w.rearrange("(k p) n -> p k n", p=P)[:, :, ds(p * P, P)])\
                      .then_inc(m_w, 16)

            def load_wo(h, p):
                for half in range(2):
                    sp.dma_start(wo_raw[h][64 * half:64 * half + 64, :], sa_wo[ds(p * P + 64 * h, 64), :])\
                      .then_inc(m_wo[h], 16)

            def place_q(h, half, signal):
                r, cols = slice(64 * h, 64 * h + 64), slice(half * BANK, (half + 1) * BANK)
                move(QKS[0:64, 3 * h, cols], QKT[r, 0, cols], signal)
                move(QKS[64:128, 3 * h, cols], QKT[r, 1, cols], signal)

            def place_k(h):
                r = slice(64 * h, 64 * h + 64)
                move(QKS[0:64, 3 * h + 1:3 * h + 3, :], QKT[r, 2:4, :], m_qk[h])
                move(QKS[64:128, 3 * h + 1:3 * h + 3, :], QKT[r, 2:4, :], m_qk[h])

            def load_v(h, p):
                move(VS[h][:, :, :], V_d[ds(2 * p + h, 1)].rearrange("a p k c -> p (a k) c"), m_v[h])

            cw = lambda w: (w[0:P, :], w[P:DC, :])
            def load_x(b):
                sp.dma_start(XN, x[ds(b, 1), :, :].rearrange("a (t p) d -> p (a t) d", p=P)).then_inc(m_x, 16)

            sp.dma_start(cnd[:, :], cond.rearrange("b t c -> (b t) c")).then_inc(m_cnd, 16)
            for dst, src in ((wk_a, cw(ca_wk)[0]), (wk_b, cw(ca_wk)[1]), (wv_a, cw(ca_wv)[0]), (wv_b, cw(ca_wv)[1])):
                sp.dma_start(dst, src).then_inc(m_kv, 16)
            sp.dma_start(X[:, :, :], ca_wo.rearrange("(n p) d -> p n d", p=P)).then_inc(m_cao, 16)
            for i, v in enumerate((sa_bo, ca_bo, ff_b2)):
                sp.dma_start(bias_row[:, i, :], v.rearrange("(a n) -> a n", a=1).broadcast_to([P, D])).then_inc(m_cst, 16)
            with nc.allow_non_contiguous_dma(reason="small vectors by feature"):
                for i, (g_, b_) in enumerate(((ln1_g, ln1_b), (ln2_g, ln2_b), (ln3_g, ln3_b))):
                    sp.dma_start(gb[:, i, 0, :], g_.rearrange("(k p) -> p k", p=P)).then_inc(m_cst, 16)
                    sp.dma_start(gb[:, i, 1, :], b_.rearrange("(k p) -> p k", p=P)).then_inc(m_cst, 16)
                sp.dma_start(b1[:, :], ff_b1.rearrange("(k p) -> p k", p=P)).then_inc(m_cst, 16)
            sp.wait_ge(s_pre, 3)
            sp.dma_start(caq, ca_wq.rearrange("(k p) n -> p k n", p=P)).then_inc(m_caq, 16)
            load_w(0)
            load_wo(0, 0)
            load_wo(1, 0)
            for i in range(16):
                sp.wait_ge(d_pre, 10 + i)
                if i == 7:
                    load_x(0)
                for l in range(2):
                    if i < 8:
                        src = PT[l][:, i % NPT, :].rearrange("p (n b c) -> p b n c", n=2, b=B)
                        for bb in range(B):
                            move(M_d[l, bb, :, i // 4, 256 * (i % 4):256 * (i % 4) + 256]
                                 .rearrange("p (n c) -> p n c", n=2), src[:, bb], m_scr[i % NPT])
                    else:
                        for bb in range(B):
                            move(VW_d[l, bb, :, i - 8, :], PT[l][:, i % NPT, 256 * bb:256 * bb + 256], m_scr[i % NPT])

            sp.wait_ge(s_pre, 25)
            sp.sem_inc(x_free, 1)

            with sp.Fori(0, B) as b:

                def moves(p, first, last):
                    g, U0 = b * NP + p, b * NU + p * UP
                    if not last:
                        wait_apart(sp, p_w, g + 2)
                        load_w_next(p)
                    if not first:
                        wait_apart(sp, s_pv, NT * U0)
                        load_v(1, p)
                    wait_apart(sp, p_wo[1], g + 1)
                    load_wo_next(1, p)
                    wait_apart(sp, p_wo[0], g + 1)
                    load_wo_next(0, p)
                    if last:
                        return
                    wait_apart(sp, d_qkv, NQ * (g + 1) + 3)
                    wait_apart(sp, s_sc, UT * (U0 + 2))
                    place_k(0)
                    place_q(0, 0, m_qk[0])
                    wait_apart(sp, d_qkv, NQ * (g + 1) + 4)
                    place_q(0, 1, m_q1[0])
                    wait_apart(sp, s_sc, UT * (U0 + 4))
                    place_k(1)
                    place_q(1, 0, m_qk[1])
                    place_q(1, 1, m_q1[1])
                    wait_apart(sp, s_pv, NT * (U0 + 2))
                    load_v(0, p + 1)

                def load_w_next(p):
                    nxt = p + 2
                    load_w(nxt if isinstance(nxt, int) and nxt < NP else (nxt % NP if isinstance(nxt, int) else nxt))

                def load_wo_next(h, p):
                    nxt = p + 1
                    load_wo(h, nxt % NP if isinstance(nxt, int) else nxt)

                wait_apart(sp, p_w, b * NP + 1)
                load_w(1)
                wait_apart(sp, d_qkv, NQ * (b * NP) + NQ)
                place_k(0)
                place_q(0, 0, m_qk[0])
                place_q(0, 1, m_q1[0])
                for i in range(NV):
                    wait_apart(sp, d_v, b * NV + i + 1)
                    move(V_d[8 * (i % 2):8 * (i % 2) + 8, :, i // 2, :].rearrange("h p c -> p h c"), vstage[i % 4], m_vst[i % 4])
                for i in range(4):
                    wait_apart(sp, m_vst[i], 16 * (NV // 4) * (b + 1))
                load_v(0, 0)
                load_v(1, 0)
                place_k(1)
                place_q(1, 0, m_qk[1])
                place_q(1, 1, m_q1[1])
                moves(0, True, False)
                with sp.Fori(1, NP - 2) as p:
                    moves(p, False, False)
                moves(NP - 2, False, False)
                moves(NP - 1, False, True)
                for i in range(NPT):
                    sp.wait_ge(m_scr[i], 64 * (16 // NPT))
                for h in range(2):
                    wait_apart(sp, m_qk[h], 64 * (b + 1) * NP)
                    wait_apart(sp, m_q1[h], 32 * (b + 1) * NP)
                for l in range(2):
                    move(Mx[l], M_d[l, ds(b, 1)].rearrange("a p k n -> p (a k) n"), m_m)
                wait_apart(sp, s_sc, UT * NU * (b + 1))
                for l in range(2):
                    move(VWx[l], VW_d[l, ds(b, 1)].rearrange("a p n d -> p (a n) d"), m_vw)
                wait_apart(sp, s_ct, 2 * NT * (b + 1))
                load_x(1 - b)
                for r in range(2):
                    wait_apart(sp, d_fx, 2 * (2 * b + r + 1))
                    sp.dma_start(out[ds(b, 1), 512 * r:512 * r + 512, :].rearrange("a (t p) d -> p (a t) d", p=P),
                                 X[:, 4 * r:4 * r + 4, :]).then_inc(m_out, 16)
                wait_apart(sp, m_out, 32 * (b + 1))
                sp.sem_inc(x_free, 1)
                wait_apart(sp, m_x, 16 * (b + 2))

        @block.gpsimd
        def _(pool):
            def split(raw, hi, lo, count):
                nc.gpsimd.tensor_copy(hi, raw).then_inc(p_wh, 1)
                pool.wait_ge(p_wh, count)
                return nc.gpsimd.tensor_tensor(lo, raw, hi.bitcast(F32), ALU.subtract)

            nc.gpsimd.memset(ident[:, :], 0.0).then_inc(p_id, 1)
            pool.wait_ge(p_id, 1)
            nc.gpsimd.affine_select(out=ident[:, :], in_=ident[:, :], compare_op=ALU.not_equal, fill=1.0,
                                    base=0, pattern=[[-1, P]], channel_multiplier=1).then_inc(p_id, 1)
            nc.gpsimd.memset(kblk, 0.0).then_inc(p_blk, 1)
            nc.gpsimd.memset(vblk, 0.0).then_inc(p_blk, 1)
            pool.wait_ge(m_w, 32)
            split(w_raw[:, :, :, :], w_s[0][:, :, :, :], w_s[1][:, :, :, :], 1).then_inc(p_w, 1)
            def load_chunk(c):
                stage = f_raw[:, c % 2, :]
                if c < 4:
                    dma = pool.dma_start(stage, sa_wv[P * (c // 2):P * (c // 2 + 1), BANK * (c % 2):BANK * (c % 2 + 1)])
                elif c < 12:
                    k, n = (c - 4) // 4, (c - 4) % 4
                    dma = pool.dma_start(stage, ff_w1[P * k:P * (k + 1), BANK * n:BANK * (n + 1)])
                else:
                    dma = pool.dma_start(stage.rearrange("p (f d) -> p f d", d=D),
                                         ff_w2[2 * P * (c - 12):2 * P * (c - 11), :].rearrange("(f p) d -> p f d", p=P))
                dma.then_inc(m_f[c % 2], 16)

            def chunk(l, c):
                if c < 4:
                    return WV[l][:, c // 2, BANK * (c % 2):BANK * (c % 2 + 1)]
                if c < 12:
                    return W1[l][:, (c - 4) // 4, BANK * ((c - 4) % 4):BANK * ((c - 4) % 4 + 1)]
                return W2[l][:, 2 * (c - 12):2 * (c - 11), :].rearrange("p f d -> p (f d)")

            load_chunk(0)
            for c in range(CHUNKS):
                if c + 1 < CHUNKS:
                    if c >= 1:
                        pool.wait_ge(p_f, c)
                    load_chunk(c + 1)
                pool.wait_ge(m_f[c % 2], 16 * (c // 2 + 1))
                done = split(f_raw[:, c % 2, :], chunk(0, c), chunk(1, c), 2 + c)
                done.then_inc(p_f, 1)
            NW0 = 1 + CHUNKS

            with pool.Fori(0, B) as b:
                def add_bias(i, r):
                    pool.wait_ge(d_z, NT * (3 * b + i) + 4 * r + 4)
                    if i == 0:
                        pool.wait_ge(m_cst, 16 * 10)
                        pool.wait_ge(x_free, b + 1)
                    rows = slice(4 * r, 4 * r + 4)
                    nc.gpsimd.tensor_tensor(X[:, rows, :], (XN if i == 0 else X)[:, rows, :],
                                            bias_row[:, i:i + 1, :].to_broadcast([P, 4, D]), ALU.add).then_inc(p_xb, 1)

                def split_wo(h, p, count):
                    g = b * NP + p
                    pool.wait_ge(m_wo[h], 32 * (g + 1))
                    if not (isinstance(p, int) and p == 0):
                        wait_apart(pool, s_op, 2 * UP * g - 4 * (1 - h))
                    else:
                        wait_apart(pool, d_z, NT * (3 * b + 1))
                    split(wo_raw[h][:, :], wo_s[h][0][:, :], wo_s[h][1][:, :], count).then_inc(p_wo[h], 1)

                def split_w(p, count):
                    g = b * NP + p
                    pool.wait_ge(m_w, 32 * (g + 1))
                    wait_apart(pool, s_qkv, NQ * g)
                    split(w_raw[:, :, :, :], w_s[0][:, :, :, :], w_s[1][:, :, :, :], count).then_inc(p_w, 1)

                per_b = 3 * NP + 4
                base = NW0 + b * per_b
                add_bias(0, 0)
                add_bias(0, 1)
                split_wo(0, 0, base + 1)
                split_w(1, base + 2)
                split_wo(1, 0, base + 3)
                with pool.Fori(1, NP - 1) as p:
                    split_wo(0, p, base + 3 * p + 1)
                    split_w(p + 1, base + 3 * p + 2)
                    split_wo(1, p, base + 3 * p + 3)
                split_wo(0, NP - 1, base + 3 * (NP - 1) + 1)
                split_wo(1, NP - 1, base + 3 * (NP - 1) + 2)
                pool.wait_ge(m_w, 32 * ((b + 1) * NP + 1))
                wait_apart(pool, s_qkv, NQ * (b + 1) * NP)
                split(w_raw[:, :, :, :], w_s[0][:, :, :, :], w_s[1][:, :, :, :], base + 3 * NP).then_inc(p_w, 1)
                add_bias(1, 0)
                for t in range(NT):
                    C = b * NT + t
                    pool.wait_ge(d_cr, C + 1)
                    e3 = E[t % 4].rearrange("p (h k) -> p h k", k=T)
                    nc.gpsimd.tensor_tensor(e3, e3, crec[:, t % 2, :].rearrange("p (h a) -> p h a", a=1)
                                            .to_broadcast([P, NH, T]), ALU.mult).then_inc(p_cn, 1)
                    if t == 2:
                        add_bias(1, 1)
                add_bias(2, 0)
                add_bias(2, 1)
                wait_apart(pool, s_co, NT * (b + 1))
                for c in range(4):
                    pool.dma_start(f_raw[:, c % 2, :], sa_wv[P * (c // 2):P * (c // 2 + 1), BANK * (c % 2):BANK * (c % 2 + 1)])\
                        .then_inc(m_f[c % 2], 16)
                    wait_apart(pool, m_f[c % 2], 16 * (CHUNKS // 2 + 2 * b + c // 2 + 1))
                    split(f_raw[:, c % 2, :], chunk(0, c), chunk(1, c), base + 3 * NP + 1 + c).then_inc(p_f, 1)

        @block.tensor
        def _(pe):
            mm = nc.tensor.matmul

            pe.wait_ge(p_id, 2)
            pe.wait_ge(m_cnd, 16)
            nc.tensor.transpose(MISC[:, 0:P], cnd[:, 0:P], ident[:, :])
            nc.tensor.transpose(MISC[0:DC - P, P:2 * P], cnd[:, P:DC], ident[:, :]).then_inc(s_pre, 1)
            pe.wait_ge(d_pre, 1)
            pe.wait_ge(m_kv, 64)
            for m, (wa, wb) in enumerate(((wk_a, wk_b), (wv_a, wv_b))):
                for q in range(2):
                    for n in range(4 * q, 4 * q + 4):
                        o = SC[m][:, n * P:(n + 1) * P]
                        mm(o, wa[:, n * P:(n + 1) * P], cndT[:, 0, :], start=True, stop=False)
                        last = mm(o, wb[:, n * P:(n + 1) * P], cndT[0:DC - P, 1, :], start=False, stop=True)
                    last.then_inc(s_pre, 1)
            pe.wait_ge(m_caq, 16)
            for i in range(4):
                bank = (TP[0], TP[1], PV, MISC)[i]
                for n in (2 * i, 2 * i + 1):
                    for k in range(KD):
                        c = (n % 2) * D + k * P
                        last = nc.tensor.transpose(bank[:, c:c + P], caq[:, k, n * P:(n + 1) * P], ident[:, :])
                last.then_inc(s_pre, 1)
            pe.wait_ge(d_pre, 9)
            for i in range(16):
                bank = SC[i // 2 % 2][:, BANK * (i % 2):BANK * (i % 2 + 1)]
                if i >= 4:
                    pe.wait_ge(d_pre, 10 + i - 4)
                if i == 8:
                    pe.wait_ge(m_cao, 16)
                for a in range(2):
                    o = bank[:, 256 * a:256 * a + 256]
                    if i < 8:
                        k, n = i // 4, 2 * (i % 4) + a
                        last = mm(o, wqT[:, n, k * P:(k + 1) * P], kblk[:, n, :, :], start=True, stop=True)
                    else:
                        last = mm(o, vblk[:, i - 8, a, :], X[:, i - 8, :], start=True, stop=True)
                last.then_inc(s_pre, 1)

            def transpose_h(L, r):
                pe.wait_ge(d_z, NT * L + 4 * r + 4)
                for k in range(2):
                    for i in range(4):
                        last = nc.tensor.transpose(HB[r][k][:, i * P:(i + 1) * P], z[:, 4 * r + i, k * P:(k + 1) * P],
                                                   ident[:, :])
                    last.then_inc(s_tr, 1)

            with pe.Fori(0, B) as b:
                def project(n, bank):
                    kind, half = PROJ[n]
                    m = "qk".index(kind)
                    for c, (l, r) in enumerate(TERMS):
                        for k in range(KD):
                            last = mm(bank[:, :], w_s[l][:, m, k, :], hT[r][:, k, half * BANK:(half + 1) * BANK],
                                      start=(c == 0 and k == 0), stop=(c == 2 and k == KD - 1))
                    last.then_inc(s_qkv, 1)

                def scores(tau):
                    h, qt = tau // 8 % 2, tau % 8
                    for half in range(2):
                        for l in range(2):
                            last = mm(SC[tau % 2][:, half * BANK:(half + 1) * BANK], QKS[:, 3 * h, qt * P:(qt + 1) * P],
                                      QKS[:, 3 * h + 1 + l, half * BANK:(half + 1) * BANK], start=(l == 0), stop=(l == 1))
                    last.then_inc(s_sc, 1)

                def attend(U, s, j):
                    h = s // 2
                    pe.wait_ge(d_pl, NT * U + j + 1)
                    for l in range(2):
                        last = mm(PV[:, :], VS[h][:, j, :], PT[l][:, j % NPT, :], start=(j == 0 and l == 0),
                                  stop=(j == NT - 1 and l == 1))
                    last.then_inc(s_pv, 1)

                def project_out(U, h, k):
                    for i in (2 * k, 2 * k + 1):
                        for c, (l, r) in enumerate(TERMS):
                            last = mm(MISC[:, D * (i % 2):D * (i % 2) + D], OT[l][:, i * P:(i + 1) * P],
                                      wo_s[h][r][:, :], start=(c == 0), stop=(c == 2))
                    last.then_inc(s_op, 1)

                for r in range(2):
                    transpose_h(3 * b, r)
                pe.wait_ge(d_hl, 4 * (3 * b) + 4)
                pe.wait_ge(p_w, b * NP + 1)
                for n in range(NQ):
                    project(n, (MISC, PV, TP[0], TP[1])[n])
                pe.wait_ge(p_f, 4 + b * CHUNKS)
                for i in range(NV):
                    bank = VB[i % 4][:, :]
                    if i < 4:
                        pe.wait_ge(d_qkv, NQ * (b * NP) + i + 1)
                    else:
                        pe.wait_ge(d_v, b * NV + i - 3)
                    for c, (l, r) in enumerate(TERMS):
                        for k in range(KD):
                            last = mm(bank, hT[l][:, k, i // 2 * P:(i // 2 + 1) * P], WV[r][:, k, i % 2 * BANK:(i % 2 + 1) * BANK],
                                      start=(c == 0 and k == 0), stop=(c == 2 and k == KD - 1))
                    last.then_inc(s_v, 1)
                    if i >= 5 and i % 2 == 1:
                        tau = (i - 5) // 2
                        if tau == 0:
                            pe.wait_ge(m_qk[0], 64 * (b * NP + 1))
                        if tau == 4:
                            pe.wait_ge(m_q1[0], 32 * (b * NP + 1))
                        if tau >= 2:
                            pe.wait_ge(a_exp, UT * NU * b + tau - 1)
                        scores(tau)
                pe.wait_ge(d_v, NV * (b + 1))

                def pair(p, first, last):
                    g, U0 = b * NP + p, b * NU + p * UP
                    for s in range(UP):
                        U = U0 + s
                        for jj in range(NT // 2):
                            if jj == 0:
                                pe.wait_ge(a_exp, UT * U + UT)
                            for j in (2 * jj, 2 * jj + 1):
                                if not (first and s == 0 and j < 2):
                                    pe.wait_ge(d_pl, NT * U + j - 1)
                                for i in range(UT):
                                    tr = nc.tensor.transpose(TP[j % 2][:, i * P:(i + 1) * P],
                                                             PR[:, s % 2, i, j * P:(j + 1) * P], ident[:, :])
                                tr.then_inc(s_pt, 1)
                            if jj == 0 and not (first and s == 0):
                                attend(U - 1, (s - 1) % UP, NT - 2)
                                attend(U - 1, (s - 1) % UP, NT - 1)
                            if jj == 1:
                                if s % 2 == 0:
                                    pe.wait_ge(m_v[s // 2], 16 * (g + 1))
                                if not (first and s == 0):
                                    pe.wait_ge(d_ol, U)
                            if jj >= 1:
                                attend(U, s, 2 * jj - 2)
                                attend(U, s, 2 * jj - 1)
                            tau = UT * s + 6 + jj
                            if not (last and tau >= 16):
                                pe.wait_ge(a_exp, UT * U0 + tau - 1)
                                if tau in (8, 16):
                                    pe.wait_ge(m_qk[tau // 8 % 2], 64 * (g + tau // 8))
                                if tau in (12, 20) or first and tau == 6:
                                    pe.wait_ge(m_q1[tau // 8 % 2], 32 * (g + max(tau // 8, 1)))
                                scores(tau)
                            if jj in (0, 3) and s < 2 and not last:
                                n = 2 * s + jj // 3
                                if n == 0:
                                    pe.wait_ge(p_w, g + 2)
                                if n in (0, 1, 3) and not (first and s == 0):
                                    pe.wait_ge(d_x, 2 * U - 2 * (n == 0))
                                elif n > 0:
                                    pe.wait_ge(d_qkv, NQ * (g + 1) + n)
                                project(n, MISC)
                            if jj in (1, 2) and not (first and s == 0):
                                if jj == 1:
                                    if s % 2 == 1:
                                        pe.wait_ge(p_wo[s // 2], g + 1)
                                    if s < 3 and not last:
                                        pe.wait_ge(d_qkv, NQ * (g + 1) + (1, 3, 4)[s])
                                    else:
                                        pe.wait_ge(d_x, 2 * U - 2)
                                else:
                                    pe.wait_ge(d_x, 2 * U - 1)
                                project_out(U - 1, (s - 1) % UP // 2, jj - 1)

                pair(0, True, False)
                with pe.Fori(1, NP - 1) as p:
                    pair(p, False, False)
                pair(NP - 1, False, True)
                UE = (b + 1) * NU
                for j in (NT - 2, NT - 1):
                    attend(UE - 1, 3, j)
                transpose_h(3 * b + 1, 0)
                pe.wait_ge(d_ol, UE)
                for k in range(2):
                    pe.wait_ge(d_x, 2 * UE - 2 + k)
                    project_out(UE - 1, 1, k)

                L2, L3 = 3 * b + 1, 3 * b + 2
                pe.wait_ge(m_m, 32 * (b + 1))
                for t in range(NT + 3):
                    C = b * NT + t
                    if t == 2:
                        transpose_h(L2, 1)
                    if t == 3:
                        pe.wait_ge(d_h, 4 * L2 + 4)
                    if t in (0, NT // 2):
                        pe.wait_ge(d_hl, 4 * L2 + (2 if t == 0 else 4))
                    if t == NT + 2:
                        transpose_h(L3, 0)
                    if t < NT:
                        if t >= 2:
                            pe.wait_ge(d_cs, C - 1)
                        for half in range(2):
                            for c, (l, r) in enumerate(TERMS):
                                for k in range(KD):
                                    last = mm(SC[t % 2][:, half * BANK:(half + 1) * BANK], hT[l][:, k, t * P:(t + 1) * P],
                                              Mx[r][:, k, half * BANK:(half + 1) * BANK],
                                              start=(c == 0 and k == 0), stop=(c == 2 and k == KD - 1))
                        last.then_inc(s_cs, 1)
                    if 2 <= t < NT + 2:
                        pe.wait_ge(p_cn, C - 1)
                        for k in range(2):
                            if t > 2:
                                pe.wait_ge(d_cl, 2 * (C - 2) + k - 1)
                            for i in range(4):
                                last = nc.tensor.transpose(TP[k][:, i * P:(i + 1) * P],
                                                           E[(t - 2) % 4][:, (4 * k + i) * P:(4 * k + i + 1) * P], ident[:, :])
                            last.then_inc(s_ct, 1)
                    if t >= 3:
                        if t == 3:
                            pe.wait_ge(m_vw, 32 * (b + 1))
                        if t >= 5:
                            pe.wait_ge(d_cx, C - 4)
                        pe.wait_ge(d_cl, 2 * (C - 3) + 2)
                        for n in range(NP):
                            for c, (l, r) in enumerate(TERMS):
                                last = mm((PV, MISC)[(t - 3) % 2][:, 0:D],
                                          PT[l][:, (2 * (t - 3) + n // 4) % NPT, (n % 4) * P:(n % 4 + 1) * P], VWx[r][:, n, :],
                                          start=(n == 0 and c == 0), stop=(n == NP - 1 and c == 2))
                        last.then_inc(s_co, 1)

                pe.wait_ge(p_f, CHUNKS)

                def ff_down(F, r, f):
                    pe.wait_ge(d_ul, F + 1)
                    for i in range(4):
                        bank = ((TP[0], TP[1]), (PV, MISC))[r][i // 2]
                        for c, (l, m) in enumerate(TERMS):
                            last = mm(bank[:, D * (i % 2):D * (i % 2) + D], PT[l][:, f % NPT, i * P:(i + 1) * P],
                                      W2[m][:, f, :], start=(f == 0 and c == 0 and i % 2 == 0),
                                      stop=(f == NF - 1 and c == 2), skip_group_check=True)
                    last.then_inc(s_w2, 1)

                for r in range(2):
                    pe.wait_ge(d_hl, 4 * L3 + 2 * r + 2)
                    for f in range(NF + 2):
                        F = b * 2 * NF + r * NF + f
                        if r == 0 and f == 2:
                            transpose_h(L3, 1)
                        if f < NF:
                            if r or f >= 2:
                                pe.wait_ge(d_u, F - 1)
                            for part, col in enumerate((FF + f * P, f * P)):
                                for c, (l, m) in enumerate(TERMS):
                                    for k in range(KD):
                                        last = mm(SC[f % 2][:, part * BANK:(part + 1) * BANK], W1[l][:, k, col:col + P],
                                                  hT[m][:, k, r * BANK:(r + 1) * BANK],
                                                  start=(c == 0 and k == 0), stop=(c == 2 and k == KD - 1))
                            last.then_inc(s_ff, 1)
                        if f >= 2:
                            ff_down(F - 2, r, f - 2)

        @block.scalar
        def _(act):
            for i in range(16):
                bank = SC[i // 2 % 2][:, BANK * (i % 2):BANK * (i % 2 + 1)]
                act.wait_ge(s_pre, 10 + i)
                if i >= NPT:
                    act.wait_ge(m_scr[i % NPT], 64 * (i // NPT))
                nc.scalar.copy(PT[0][:, i % NPT, :], bank).then_inc(a_pre, 1)

            for i in range(NPT):
                act.wait_ge(m_scr[i], 64 * (16 // NPT))
            with act.Fori(0, B) as b:
                def root(L, r):
                    act.wait_ge(d_mv, NT * L + 4 * r + 4)
                    nc.scalar.activation(sd[:, 4 * r:4 * r + 4], mv[:, 4 * r:4 * r + 4, 1], ACT.Sqrt, bias=EPS)\
                        .then_inc(a_sd, 1)

                def split_h(L, r):
                    for k in range(2):
                        act.wait_ge(d_h, 4 * L + 2 * r + k + 1)
                        nc.scalar.copy(hT[0][:, k, r * BANK:(r + 1) * BANK], h32[:, k, r * BANK:(r + 1) * BANK]).then_inc(a_hh, 1)

                def split_qkv(g, n, bank):
                    kind, half = PROJ[n]
                    act.wait_ge(s_qkv, NQ * g + n + 1)
                    nc.scalar.mul(QKT[:, 2 * "qk".index(kind), half * BANK:(half + 1) * BANK], bank[:, :],
                                  SCALE if kind == "q" else 1.0).then_inc(a_qkv, 1)

                def exp(U0, tau):
                    u = tau // UT
                    act.wait_ge(d_max, UT * U0 + tau + 1)
                    nc.scalar.activation(PR[:, u % 2, tau % UT, :], SC[tau % 2][:, :], ACT.Exp,
                                         bias=nmax[:, tau % 4:tau % 4 + 1],
                                         accum_out=den[:, u % 2, tau % UT:tau % UT + 1]).then_inc(a_exp, 1)

                def split_out(U, first):
                    act.wait_ge(s_pv, NT * U + NT)
                    if not first:
                        act.wait_ge(s_op, 2 * U)
                    nc.scalar.copy(OT[0][:, :], PV[:, :]).then_inc(a_oh, 1)

                for step in (root, split_h):
                    for r in range(2):
                        step(3 * b, r)
                for n in range(NQ):
                    split_qkv(b * NP, n, (MISC, PV, TP[0], TP[1])[n])
                for i in range(NV):
                    act.wait_ge(s_v, b * NV + i + 1)
                    if i >= 4:
                        act.wait_ge(m_vst[i % 4], 16 * (b * (NV // 4) + i // 4))
                    nc.scalar.copy(vstage[i % 4][:, :, 0:DH],
                                   VB[i % 4][:, :].rearrange("p (h d) -> p h d", d=DH)).then_inc(a_v, 1)
                    if i >= 6 and i % 2 == 0:
                        if i == 14:
                            act.wait_ge(p_xb, 6 * b + 2)
                        exp(b * NU, (i - 6) // 2)

                def pair(p, first, last):
                    g, U0 = b * NP + p, b * NU + p * UP
                    for s in range(UP):
                        U = U0 + s
                        for jj in range(NT // 2):
                            if not last and ((s < 2 and jj == 1) or (1 <= s < 3 and jj == 0)):
                                n = 2 * s - 1 + jj
                                if n == 0:
                                    for h in range(2):
                                        act.wait_ge(m_qk[h], 64 * (g + 1))
                                        act.wait_ge(m_q1[h], 32 * (g + 1))
                                split_qkv(g + 1, n, MISC)
                            for j in (2 * jj, 2 * jj + 1):
                                act.wait_ge(s_pt, NT * U + j + 1)
                                if not (first and s == 0 and j < NPT):
                                    act.wait_ge(s_pv, NT * U + j - NPT + 1)
                                nc.scalar.copy(PT[0][:, j % NPT, :], TP[j % 2][:, :]).then_inc(a_ph, 1)
                            if jj == 0 and not (first and s == 0):
                                split_out(U - 1, first and s == 1)
                            tau = UT * s + 5 + jj
                            if not (last and tau >= 16):
                                if jj == 3:
                                    act.wait_ge(d_rd, U + 1)
                                exp(U0, tau)

                pair(0, True, False)
                with act.Fori(1, NP - 1) as p:
                    pair(p, False, False)
                pair(NP - 1, False, True)
                L2, L3 = 3 * b + 1, 3 * b + 2
                root(L2, 0)
                split_out((b + 1) * NU - 1, False)
                split_h(L2, 0)
                root(L2, 1)
                for t in range(NT + 3):
                    C = b * NT + t
                    if t < NT:
                        act.wait_ge(d_cs, C + 1)
                        nc.scalar.activation(E[t % 4], E[t % 4], ACT.Exp).then_inc(a_ce, 1)
                    if t == 1:
                        split_h(L2, 1)
                    if t == NT + 1:
                        root(L3, 0)
                    if t == NT + 2:
                        split_h(L3, 0)
                    if 2 <= t < NT + 2:
                        for k in range(2):
                            act.wait_ge(s_ct, 2 * (C - 2) + k + 1)
                            if t >= 4:
                                act.wait_ge(s_co, C - 3)
                            nc.scalar.copy(PT[0][:, (2 * (t - 2) + k) % NPT, :], TP[k][:, :]).then_inc(a_ch, 1)

                root(L3, 1)
                for r in range(2):
                    for f in range(NF + 1):
                        F = b * 2 * NF + r * NF + f
                        if f < NF:
                            act.wait_ge(s_ff, F + 1)
                            if r or f >= 2:
                                act.wait_ge(d_u, F - 1)
                            nc.scalar.activation(G[f % 2], SC[f % 2][:, 0:BANK], ACT.Gelu,
                                                 bias=b1[:, NF + f:NF + f + 1]).then_inc(a_g, 1)
                        if f >= 1:
                            act.wait_ge(d_u, F)
                            if r or f - 1 >= NPT:
                                act.wait_ge(s_w2, F - NPT)
                            nc.scalar.copy(PT[0][:, (f - 1) % NPT, :], U32[(f - 1) % 2]).then_inc(a_uh, 1)
                        if r == 0 and f == 1:
                            split_h(L3, 1)

        @block.vector
        def _(dve):
            V = nc.vector
            sub = ALU.subtract

            dve.wait_ge(s_pre, 1)
            V.tensor_copy(cndT[:, 0, :], MISC[:, 0:P])
            V.tensor_copy(cndT[0:DC - P, 1, :], MISC[0:DC - P, P:2 * P]).then_inc(d_pre, 1)
            dve.wait_ge(p_blk, 2)
            for m, blk in enumerate((kblk, vblk)):
                for q in range(2):
                    dve.wait_ge(s_pre, 2 + 2 * m + q)
                    for h in range(2):
                        rows = slice(64 * h, 64 * h + 64)
                        src = SC[m][rows, q * BANK:(q + 1) * BANK].rearrange("p (n b c) -> p n b c", n=4, b=B)
                        last = V.tensor_scalar(blk[rows, 4 * q:4 * q + 4, :, 64 * h:64 * h + 64], src,
                                               (SCALE, 1.0)[m], None, ALU.mult)
                    last.then_inc(d_pre, 1)
            for i in range(4):
                dve.wait_ge(s_pre, 6 + i)
                V.tensor_copy(wqT[:, 2 * i:2 * i + 2, :].rearrange("p n c -> p (n c)"),
                              (TP[0], TP[1], PV, MISC)[i][:, :]).then_inc(d_pre, 1)
            for i in range(16):
                bank = SC[i // 2 % 2][:, BANK * (i % 2):BANK * (i % 2 + 1)]
                dve.wait_ge(a_pre, i + 1)
                V.tensor_tensor(PT[1][:, i % NPT, :], bank, PT[0][:, i % NPT, :].bitcast(F32), sub).then_inc(d_pre, 1)

            with dve.Fori(0, B) as b:
                def stats(L, tiles, src):
                    for t in tiles:
                        V.bn_stats(st[:, t, :], src[:, t, :]).then_inc(d_st, 1)
                    wait_apart(dve, d_st, NT * L + tiles[-1] + 1)
                    for t in tiles:
                        V.bn_aggr(mv[:, t, :], st[:, t, :]).then_inc(d_mv, 1)

                def scale(L, r, src):
                    rows = slice(4 * r, 4 * r + 4)
                    dve.wait_ge(a_sd, 2 * L + r + 1)
                    V.reciprocal(rs[:, rows], sd[:, rows]).then_inc(d_rs, 1)
                    dve.wait_ge(d_rs, 2 * L + r + 1)
                    for t in range(4 * r, 4 * r + 4):
                        V.tensor_scalar(z[:, t, :], src[:, t, :], mv[:, t, 0:1], rs[:, t:t + 1], sub, ALU.mult).then_inc(d_z, 1)

                def gain(L, r, i):
                    for k in range(2):
                        dve.wait_ge(s_tr, 4 * L + 2 * r + k + 1)
                        V.tensor_scalar(h32[:, k, r * BANK:(r + 1) * BANK], HB[r][k], gb[:, i, 0, k:k + 1],
                                        gb[:, i, 1, k:k + 1], ALU.mult, ALU.add).then_inc(d_h, 1)

                def split_h(L, r):
                    for k in range(2):
                        dve.wait_ge(a_hh, 4 * L + 2 * r + k + 1)
                        V.tensor_tensor(hT[1][:, k, r * BANK:(r + 1) * BANK], h32[:, k, r * BANK:(r + 1) * BANK],
                                        hT[0][:, k, r * BANK:(r + 1) * BANK].bitcast(F32), sub).then_inc(d_hl, 1)

                def split_qkv(g, n, bank):
                    kind, half = PROJ[n]
                    dve.wait_ge(a_qkv, NQ * g + n + 1)
                    m, cols = 2 * "qk".index(kind), slice(half * BANK, (half + 1) * BANK)
                    V.scalar_tensor_tensor(QKT[:, m + 1, cols], bank[:, :], SCALE if kind == "q" else 1.0,
                                           QKT[:, m, cols].bitcast(F32), ALU.mult, sub).then_inc(d_qkv, 1)

                def rowmax(U0, tau, fresh):
                    dve.wait_ge(s_sc, UT * U0 + tau + 1)
                    if not fresh:
                        dve.wait_ge(a_exp, UT * U0 + tau - 3)
                    V.tensor_reduce(nmax[:, tau % 4:tau % 4 + 1], SC[tau % 2][:, :], AX, ALU.max, negate=True).then_inc(d_max, 1)

                def split_out(U):
                    dve.wait_ge(a_oh, U + 1)
                    V.tensor_tensor(OT[1][:, :], PV[:, :], OT[0][:, :].bitcast(F32), sub).then_inc(d_ol, 1)

                def add_out(U, s, k):
                    dve.wait_ge(s_op, 2 * U + k + 1)
                    for i in (2 * k, 2 * k + 1):
                        t = UT * (s % 2) + i
                        last = V.scalar_tensor_tensor(X[:, t, :], MISC[:, D * (i % 2):D * (i % 2) + D],
                                                      rden[:, s % 2, i:i + 1], X[:, t, :], ALU.mult, ALU.add)
                    last.then_inc(d_x, 1)

                dve.wait_ge(m_x, 16 * (b + 1))
                dve.wait_ge(m_cst, 160)
                stats(3 * b, range(NT), XN)
                for r in range(2):
                    scale(3 * b, r, XN)
                for r in range(2):
                    gain(3 * b, r, 0)
                for r in range(2):
                    split_h(3 * b, r)
                for n in range(NQ):
                    split_qkv(b * NP, n, (MISC, PV, TP[0], TP[1])[n])
                for i in range(NV):
                    dve.wait_ge(a_v, b * NV + i + 1)
                    V.tensor_tensor(vstage[i % 4][:, :, DH:P],
                                    VB[i % 4][:, :].rearrange("p (h d) -> p h d", d=DH),
                                    vstage[i % 4][:, :, 0:DH].bitcast(F32), sub).then_inc(d_v, 1)
                    if i >= 5 and i % 2 == 1:
                        rowmax(b * NU, (i - 5) // 2, i < 13)
                dve.wait_ge(p_xb, 6 * b + 2)

                def pair(p, first, last):
                    g, U0 = b * NP + p, b * NU + p * UP
                    for s in range(UP):
                        U = U0 + s
                        for jj in range(NT // 2):
                            if not last and ((s < 2 and jj == 1) or (1 <= s < 3 and jj == 0)):
                                split_qkv(g + 1, 2 * s - 1 + jj, MISC)
                            if jj >= 2 and not (first and s == 0):
                                add_out(U - 1, (s - 1) % UP, jj - 2)
                            for j in (2 * jj, 2 * jj + 1):
                                dve.wait_ge(a_ph, NT * U + j + 1)
                                V.tensor_tensor(PT[1][:, j % NPT, :], TP[j % 2][:, :], PT[0][:, j % NPT, :].bitcast(F32),
                                                sub).then_inc(d_pl, 1)
                            if jj == 0:
                                if not (first and s == 0):
                                    split_out(U - 1)
                                dve.wait_ge(a_exp, UT * U + UT)
                                if not (first and s < 2):
                                    dve.wait_ge(d_x, 2 * U - 2)
                                V.reciprocal(rden[:, s % 2, :], den[:, s % 2, :]).then_inc(d_rd, 1)
                            tau = UT * s + 6 + jj
                            if not (last and tau >= 16):
                                rowmax(U0, tau, False)
                            if last and s == 3 and jj == 3:
                                dve.wait_ge(d_x, 2 * U)
                                stats(3 * b + 1, range(NT // 2), X)

                pair(0, True, False)
                with dve.Fori(1, NP - 1) as p:
                    pair(p, False, False)
                pair(NP - 1, False, True)
                L2, L3 = 3 * b + 1, 3 * b + 2
                scale(L2, 0, X)
                split_out((b + 1) * NU - 1)
                gain(L2, 0, 1)
                add_out((b + 1) * NU - 1, 3, 0)
                split_h(L2, 0)
                add_out((b + 1) * NU - 1, 3, 1)
                dve.wait_ge(d_x, 2 * NU * (b + 1))
                stats(L2, range(NT // 2, NT), X)
                for t in range(NT + 3):
                    C = b * NT + t
                    if t < NT:
                        ps3 = SC[t % 2][:, :].rearrange("p (h k) -> p h k", k=T)
                        bc = lambda v: v[:, t % 2, :].rearrange("p (h a) -> p h a", a=1).to_broadcast([P, NH, T])
                        dve.wait_ge(s_cs, C + 1)
                        V.tensor_reduce(cmax[:, t % 2, :], ps3, AX, ALU.max).then_inc(d_cm, 1)
                        dve.wait_ge(d_cm, C + 1)
                        if t >= 4:
                            dve.wait_ge(s_ct, 2 * (C - 3))
                        V.tensor_tensor(E[t % 4].rearrange("p (h k) -> p h k", k=T), ps3, bc(cmax), sub).then_inc(d_cs, 1)
                    if t == 0:
                        scale(L2, 1, X)
                    if 1 <= t < NT + 1:
                        dve.wait_ge(a_ce, C)
                        V.tensor_reduce(csum[:, (t - 1) % 2, :], E[(t - 1) % 4].rearrange("p (h k) -> p h k", k=T),
                                        AX, ALU.add).then_inc(d_csum, 1)
                        dve.wait_ge(d_csum, C)
                        if t >= 3:
                            dve.wait_ge(p_cn, C - 2)
                        V.reciprocal(crec[:, (t - 1) % 2, :], csum[:, (t - 1) % 2, :]).then_inc(d_cr, 1)
                    if 2 <= t < NT + 2:
                        for k in range(2):
                            dve.wait_ge(a_ch, 2 * (C - 2) + k + 1)
                            slot = (2 * (t - 2) + k) % NPT
                            V.tensor_tensor(PT[1][:, slot, :], TP[k][:, :], PT[0][:, slot, :].bitcast(F32), sub).then_inc(d_cl, 1)
                    if t == 1:
                        gain(L2, 1, 1)
                        split_h(L2, 1)
                    if t == NT:
                        dve.wait_ge(d_cx, b * NT + NT // 2)
                        stats(L3, range(NT // 2), X)
                    if t == NT + 1:
                        scale(L3, 0, X)
                    if t == NT + 2:
                        gain(L3, 0, 2)
                        split_h(L3, 0)
                    if t >= 3:
                        if t in (3, 3 + NT // 2):
                            dve.wait_ge(p_xb, 6 * b + 3 + t // 5)
                        dve.wait_ge(s_co, C - 2)
                        V.tensor_tensor(X[:, t - 3, :], (PV, MISC)[(t - 3) % 2][:, 0:D], X[:, t - 3, :], ALU.add).then_inc(d_cx, 1)
                dve.wait_ge(d_cx, NT * (b + 1))

                stats(L3, range(NT // 2, NT), X)
                scale(L3, 1, X)
                for r in range(2):
                    for f in range(NF + 1):
                        F = b * 2 * NF + r * NF + f
                        if f < NF:
                            dve.wait_ge(a_g, F + 1)
                            if r or f >= 2:
                                dve.wait_ge(d_ul, F - 1)
                            V.scalar_tensor_tensor(U32[f % 2], SC[f % 2][:, BANK:2 * BANK], b1[:, f:f + 1], G[f % 2],
                                                   ALU.add, ALU.mult).then_inc(d_u, 1)
                        if f >= 1:
                            dve.wait_ge(a_uh, F)
                            V.tensor_tensor(PT[1][:, (f - 1) % NPT, :], U32[(f - 1) % 2],
                                            PT[0][:, (f - 1) % NPT, :].bitcast(F32), sub).then_inc(d_ul, 1)
                        if r == 0 and f == 1:
                            gain(L3, 1, 2)
                            split_h(L3, 1)
                    dve.wait_ge(p_xb, 6 * b + 5 + r)
                    dve.wait_ge(s_w2, NF * (2 * b + r + 1))
                    for i in range(2):
                        xs = X[:, 4 * r + 2 * i:4 * r + 2 * i + 2, :].rearrange("p t d -> p (t d)")
                        V.tensor_tensor(xs, ((TP[0], TP[1]), (PV, MISC))[r][i][:, :], xs, ALU.add).then_inc(d_fx, 1)


_INS = ['x', 'ctx_768'] + ['L0_xattn_' + n for n in (
    'ln1_g', 'ln1_b', 'ln2_g', 'ln2_b', 'ln3_g', 'ln3_b', 'sa_wq', 'sa_wk', 'sa_wv', 'sa_wo', 'sa_bo',
    'ca_wq', 'ca_wk', 'ca_wv', 'ca_wo', 'ca_bo', 'ff_w1', 'ff_b1', 'ff_w2', 'ff_b2')]
_OUTS = [((2, 1024, 256), 'float32')]


def kernel(**inputs):
    import numpy as _np
    import concourse.bacc as _bacc
    from concourse import mybir as _mybir
    from concourse.bass_utils import run_bass_kernel_spmd as _run

    nc = _bacc.Bacc("TRN2", target_bir_lowering=False, num_devices=1)
    arrays, args = {}, []
    for name in _INS:
        a = _np.ascontiguousarray(inputs[name])
        arrays[f"in_{name}_dram"] = a
        args.append(nc.dram_tensor(f"in_{name}_dram", a.shape, _mybir.dt.from_np(a.dtype), kind="ExternalInput").ap())
    for i, (shape, dtype) in enumerate(_OUTS):
        dt = _mybir.dt.from_np(_np.dtype(dtype))
        args.append(nc.dram_tensor(f"out_{i}_dram", shape, dt, kind="ExternalOutput").ap())
    build_block(nc, *args)
    r = _run(nc, [arrays], core_ids=[0])
    got = tuple(r.results[0][f"out_{i}_dram"] for i in range(len(_OUTS)))
    return got[0]
```
